# Optimizing a Trainium2 kernel written in Bass

```python
import numpy as np
import jax
import jax.numpy as jnp

def _softmax(x, axis=-1):
    return jax.nn.softmax(x, axis=axis)

def _gelu(x):
    return jax.nn.gelu(x, approximate=True)

def _silu(x):
    return jax.nn.silu(x)

def _sigmoid(x):
    return jax.nn.sigmoid(x)

def _layernorm(x, axis=-1, eps=1e-05):
    m = jnp.mean(x, axis=axis, keepdims=True)
    v = jnp.var(x, axis=axis, keepdims=True)
    return (x - m) / jnp.sqrt(v + eps)

def _scatter_add(tgt, idx, src, axis=0):
    return tgt.at[idx].add(src)

def _segment_sum(src, seg, n):
    return jax.ops.segment_sum(src, seg, n)
kernel_name = 'mk_flamingo_gated_d1_seqx_r4_c63e45'

def setup_inputs(seed: int=0):
    np.random.seed(seed)
    _w = jnp.asarray

    def _rec_inputs():
        import jax
        import jax.numpy as jnp
        _rk = jax.random.key(seed)
        x = -0.0002928 + 1 * jax.random.normal(jax.random.fold_in(_rk, 1), (64, 128, 256), jnp.float32)
        _lenS = 128 - jax.random.randint(jax.random.fold_in(_rk, 7), (64,), 0, max(1, 128 // 4) + 1, jnp.int32)
        _lenS2 = 128 - jax.random.randint(jax.random.fold_in(_rk, 8), (64,), 0, max(1, 128 // 4) + 1, jnp.int32)
        _ctx_1024P = jax.random.normal(jax.random.fold_in(_rk, 11), (64, 16, 256), jnp.float32)
        _ctx_1024c = jax.random.dirichlet(jax.random.fold_in(_rk, 511), 0.3 * jnp.ones((16,), jnp.float32), (64, 128))
        _ctx_1024t = jnp.einsum('bsk,bkd->bsd', _ctx_1024c, _ctx_1024P)
        _ctx_1024t = _ctx_1024t * jax.lax.rsqrt(jnp.mean(jnp.square(_ctx_1024t)) + 1e-12) * 0.953939
        ctx_1024 = -1.39393e-06 + 0.999914 * (_ctx_1024t + 0.3 * jax.random.normal(jax.random.fold_in(_rk, 611), (64, 128, 256), jnp.float32))
        _g = jax.random.normal(jax.random.fold_in(_rk, 9001), (2, 1), jnp.float32)
        _g = jnp.sign(_g) * jnp.maximum(jnp.abs(_g), 1.0) + (_g == 0) * 1.0
        g_xattn = _g[0]
        g_ffn = _g[1]
        return (x, ctx_1024, g_xattn, g_ffn)
    x, ctx_1024, g_xattn, g_ffn = _rec_inputs()

    def _L0_xattn_setup():
        import jax, jax.numpy as jnp
        import numpy as np
        B, S, E = (2, 512, 256)
        H = 16
        D = E // H
        key = jax.random.key(seed)
        ks = jax.random.split(key, 8)
        scale = 1.0 / np.sqrt(E)
        return {'q': jax.random.normal(ks[0], (B, S, E), dtype=jnp.float32), 'k': jax.random.normal(ks[1], (B, S, E), dtype=jnp.float32), 'v': jax.random.normal(ks[2], (B, S, E), dtype=jnp.float32), 'Wq': jax.random.normal(ks[3], (H, E, D), dtype=jnp.float32) * scale, 'Wk': jax.random.normal(ks[4], (H, E, D), dtype=jnp.float32) * scale, 'Wv': jax.random.normal(ks[5], (H, E, D), dtype=jnp.float32) * scale, 'Wo': jax.random.normal(ks[6], (E, E), dtype=jnp.float32) * scale, 'bo': jax.random.normal(ks[7], (E,), dtype=jnp.float32) * 0.01}
    _L0_xattn_all = _L0_xattn_setup()
    _L0_xattn_in = {k: v for k, v in _L0_xattn_all.items() if k in ('Wq', 'Wk', 'Wv', 'Wo', 'bo')}
    del _L0_xattn_all

    def _L0_ffn_setup():
        import jax, jax.numpy as jnp
        import numpy as np
        D_IN, D_HID = (256, 1024)

        def _ternary(key, shape):
            return jax.random.randint(key, shape, -1, 2).astype(jnp.float32)

        def _tlin(x, w, s):
            return jnp.einsum('bsi,oi->bso', x, w) * s
        key = jax.random.key(seed)
        ks = jax.random.split(key, 12)
        inv = lambda fan: 1.0 / np.sqrt(fan).astype(np.float32)
        return {'x': jax.random.normal(ks[0], (4, 512, D_IN), dtype=jnp.float32), 'w1_w': _ternary(ks[1], (D_HID, D_IN)), 'w1_s': jax.random.uniform(ks[2], (D_HID,), dtype=jnp.float32) * inv(D_IN), 'w2_w': _ternary(ks[3], (D_HID, D_IN)), 'w2_s': jax.random.uniform(ks[4], (D_HID,), dtype=jnp.float32) * inv(D_IN), 'h1_w': _ternary(ks[5], (D_HID, D_HID)), 'h1_s': jax.random.uniform(ks[6], (D_HID,), dtype=jnp.float32) * inv(D_HID), 'h2_w': _ternary(ks[7], (D_HID, D_HID)), 'h2_s': jax.random.uniform(ks[8], (D_HID,), dtype=jnp.float32) * inv(D_HID), 'w3_w': _ternary(ks[9], (D_IN, D_HID)), 'w3_s': jax.random.uniform(ks[10], (D_IN,), dtype=jnp.float32) * inv(D_HID)}
    _L0_ffn_all = _L0_ffn_setup()
    _L0_ffn_in = {k: v for k, v in _L0_ffn_all.items() if k in ('w1_w', 'w1_s', 'w2_w', 'w2_s', 'h1_w', 'h1_s', 'h2_w', 'h2_s', 'w3_w', 'w3_s')}
    del _L0_ffn_all
    return {'x': x, 'ctx_1024': ctx_1024, 'g_xattn': g_xattn, 'g_ffn': g_ffn, 'L0_xattn_Wq': _L0_xattn_in['Wq'], 'L0_xattn_Wk': _L0_xattn_in['Wk'], 'L0_xattn_Wv': _L0_xattn_in['Wv'], 'L0_xattn_Wo': _L0_xattn_in['Wo'], 'L0_xattn_bo': _L0_xattn_in['bo'], 'L0_ffn_w1_w': _L0_ffn_in['w1_w'], 'L0_ffn_w1_s': _L0_ffn_in['w1_s'], 'L0_ffn_w2_w': _L0_ffn_in['w2_w'], 'L0_ffn_w2_s': _L0_ffn_in['w2_s'], 'L0_ffn_h1_w': _L0_ffn_in['h1_w'], 'L0_ffn_h1_s': _L0_ffn_in['h1_s'], 'L0_ffn_h2_w': _L0_ffn_in['h2_w'], 'L0_ffn_h2_s': _L0_ffn_in['h2_s'], 'L0_ffn_w3_w': _L0_ffn_in['w3_w'], 'L0_ffn_w3_s': _L0_ffn_in['w3_s']}

def reference(x, ctx_1024, g_xattn, g_ffn, L0_xattn_Wq, L0_xattn_Wk, L0_xattn_Wv, L0_xattn_Wo, L0_xattn_bo, L0_ffn_w1_w, L0_ffn_w1_s, L0_ffn_w2_w, L0_ffn_w2_s, L0_ffn_h1_w, L0_ffn_h1_s, L0_ffn_h2_w, L0_ffn_h2_s, L0_ffn_w3_w, L0_ffn_w3_s):
    import jax
    import jax.numpy as jnp

    def _L0_xattn_ref(q, k, v, Wq, Wk, Wv, Wo, bo):
        import jax, jax.numpy as jnp
        import numpy as np
        B, S, E = (2, 512, 256)
        H = 16
        D = E // H
        d = Wq.shape[-1]
        qh = jnp.einsum('bse,hed->bhsd', q, Wq)
        kh = jnp.einsum('bse,hed->bhsd', k, Wk)
        vh = jnp.einsum('bse,hed->bhsd', v, Wv)
        scores = jnp.einsum('bhsd,bhtd->bhst', qh, kh) / jnp.sqrt(jnp.asarray(d, dtype=qh.dtype))
        s = q.shape[1]
        causal = jnp.tril(jnp.ones((s, s), dtype=bool))
        scores = jnp.where(causal, scores, jnp.asarray(-1000000000.0, dtype=scores.dtype))
        att = jax.nn.softmax(scores, axis=-1)
        out = jnp.einsum('bhst,bhtd->bhsd', att, vh)
        concat = out.transpose(0, 2, 1, 3).reshape(q.shape[0], s, -1)
        return concat @ Wo.T + bo

    def _L0_ffn_ref(x, w1_w, w1_s, w2_w, w2_s, h1_w, h1_s, h2_w, h2_s, w3_w, w3_s):
        import jax, jax.numpy as jnp
        import numpy as np
        D_IN, D_HID = (256, 1024)

        def _ternary(key, shape):
            return jax.random.randint(key, shape, -1, 2).astype(jnp.float32)

        def _tlin(x, w, s):
            return jnp.einsum('bsi,oi->bso', x, w) * s
        h = jax.nn.silu(_tlin(x, w1_w, w1_s)) * _tlin(x, w2_w, w2_s)
        h = jax.nn.gelu(_tlin(h, h1_w, h1_s), approximate=False)
        h = jax.nn.gelu(_tlin(h, h2_w, h2_s), approximate=False)
        return _tlin(h, w3_w, w3_s)
    x = x + jnp.tanh(g_xattn[0]) * _L0_xattn_ref(_layernorm(x, axis=-1), ctx_1024, ctx_1024, L0_xattn_Wq, L0_xattn_Wk, L0_xattn_Wv, L0_xattn_Wo, L0_xattn_bo)
    x = x + jnp.tanh(g_ffn[0]) * _L0_ffn_ref(_layernorm(x, axis=-1), L0_ffn_w1_w, L0_ffn_w1_s, L0_ffn_w2_w, L0_ffn_w2_s, L0_ffn_h1_w, L0_ffn_h1_s, L0_ffn_h2_w, L0_ffn_h2_s, L0_ffn_w3_w, L0_ffn_w3_s)
    return x

_drawn_inputs = setup_inputs


def setup_inputs(seed=0):
    import zlib

    import numpy as np

    out = dict(_drawn_inputs(seed))
    spreads = {}
    factors = {}
    for name, (base, spread) in spreads.items():
        noise = np.random.default_rng([zlib.crc32(name.encode()), seed]).standard_normal(out[name].shape)
        drawn = base * np.exp(spread * noise) if base else spread * noise
        out[name] = jnp.asarray(drawn.astype(out[name].dtype))
    for name, factor in factors.items():
        out[name] = (out[name] * factor).astype(out[name].dtype)
    return out
```

```python
from contextlib import ExitStack

import concourse.bass as bass
from concourse import mybir

ALU = mybir.AluOpType
ACT = mybir.ActivationFunctionType
F32 = mybir.dt.float32
F32R = mybir.dt.float32r
I32 = mybir.dt.int32
AX_X = mybir.AxisListType.X

P = 128
ROWS = 2
TOK = ROWS * P
BANK = 512
LOW_BITS = 0xFFF
MASKED = -1e9
EPS = 1e-5

G_ORDER = [("To", 0), ("L2", 0), ("To", 1), ("O", 0), ("L2", 1), ("O", 1), ("N2", 0), ("L2", 2), ("X2", 0),
           ("N2", 1), ("L2", 3), ("X2", 1), ("x", 0), ("L3", 0), ("c", 0), ("L3", 1), ("Q", 0), ("L3", 2),
           ("K", 0), ("L3", 3), ("V", 0), ("V", 1), ("L4", 0), ("L4", 1)]
FFN_KINDS = ("L2", "L3", "L4")
HEAD_KINDS = ("x", "c", "Q", "K", "V")
WORK_STEPS = [s for s in G_ORDER if s[0] not in FFN_KINDS and s[0] != "N2"]
HEAD_STEPS = [s for s in WORK_STEPS if s[0] in HEAD_KINDS]
WORK_TAIL = len(WORK_STEPS) - len(HEAD_STEPS)


def program(nc, x, ctx_in, g_xattn, g_ffn, Wq, Wk, Wv, Wo, bo, w1, s1, w2, s2, h1, h1s, h2, h2s, w3, w3s, out):
    B, S, E = x.shape
    H, _, D = Wq.shape
    F = w1.shape[0]
    BLOCKS = B // ROWS
    KE = E // P
    KF = F // P
    NQ = ROWS * H // 4
    QROW = H // 4
    HPT = P // D
    SCALE = 1.0 / float(D) ** 0.5
    PAIRS = KF // 2
    assert S == P and H * D == E and KE == 2 and KF == NQ == 8 and QROW == 2 * KE

    W1_AT, W2_AT, H1_AT = 0, KE * F, 2 * KE * F
    H2_AT, W3_AT = H1_AT + KF * F, H1_AT + 2 * KF * F
    W_COLS = W3_AT + KF * E

    CHUNK = 4 * BANK
    chunks = []
    for w, at in ((w1, W1_AT), (w2, W2_AT)):
        chunks.append((w.rearrange("(o p) e -> p o e", p=P),
                       [([(4 * q + r, kt * P) for r in range(4)], at + kt * F + 4 * q * P)
                        for q in range(2) for kt in range(KE)]))
    for w, at in ((h1, H1_AT), (h2, H2_AT)):
        for q in range(2):
            for c in range(2):
                src = w[q * BANK:(q + 1) * BANK, c * BANK:(c + 1) * BANK].rearrange("(o p) e -> p o e", p=P)
                chunks.append((src, [([(r, k * P) for r in range(4)], at + (4 * c + k) * F + 4 * q * P)
                                     for k in range(4)]))
    chunks.append((w3.rearrange("(o p) e -> p o e", p=P),
                   [([(0, kt * P), (1, kt * P), (0, (kt + 1) * P), (1, (kt + 1) * P)], W3_AT + kt * E)
                    for kt in range(0, KF, 2)]))
    CHUNKS = len(chunks)
    groups = [(c, tiles, at) for c, (_, gs) in enumerate(chunks) for tiles, at in gs]
    GROUPS = len(groups)
    SLOTS = NQ + 3
    assert CHUNKS == SLOTS

    with ExitStack() as ctx:
        def sb(name, shape, dt=F32):
            return ctx.enter_context(nc.sbuf_tensor(name, shape, dt))

        def bank(name):
            return ctx.enter_context(nc.psum_tensor(name, [P, BANK], F32))

        def sem(name):
            return ctx.enter_context(nc.semaphore(name))

        W = sb("W", [P, W_COLS], F32R)
        wq = sb("wq", [P, KE, E])
        wk = sb("wk", [P, KE, E])
        wv = sb("wv", [P, KE, E])
        wo_nat = sb("wo_nat", [P, KE, E])
        woT = sb("woT", [P, KE, E])
        ident = sb("ident", [P, P])
        causal = sb("causal", [P, 4, P])
        headmask = sb("headmask", [P, HPT])
        bo_tg = sb("bo_tg", [P, E])
        s3_tg = sb("s3_tg", [P, E])
        gates_in = sb("gates_in", [P, 2])
        gates = sb("gates", [P, 2])
        s1_col = sb("s1_col", [P, KF])
        s2_col = sb("s2_col", [P, KF])
        half_s1 = sb("half_s1", [P, KF])
        half_s12 = sb("half_s12", [P, KF])
        h1s_col = sb("h1s_col", [P, KF])
        h2s_col = sb("h2s_col", [P, KF])
        minus_half = sb("minus_half", [P, ROWS])
        ones = sb("ones", [P, 1])
        low_max = sb("low_max", [P, CHUNKS], I32)
        low_all = sb("low_all", [P, 1], I32)
        inexact = sb("inexact", [P, 1])
        flag = sb("flag", [1, 1], I32)

        x_in = sb("x_in", [P, ROWS, E])
        c_in = sb("c_in", [P, ROWS, E])
        stats = sb("stats", [P, ROWS, 6])
        moments = sb("moments", [P, ROWS, 2])
        var_eps = sb("var_eps", [P, ROWS])
        rstd = sb("rstd", [P, ROWS])
        xn = sb("xn", [P, ROWS, E])
        xres = sb("xres", [P, ROWS, E])
        xT = sb("xT", [P, KE, TOK])
        cT = sb("cT", [P, KE, TOK])
        qT = sb("qT", [P, KE, TOK])
        kT = sb("kT", [P, KE, TOK])
        KSLOTS = 2
        kbd = sb("kbd", [P, KSLOTS, HPT, P])
        v1 = sb("v1", [P, ROWS, H, D + 1])
        PSLOTS = 4
        probs = sb("probs", [P, PSLOTS, 4, P])
        negmax = sb("negmax", [P, PSLOTS, 4])
        pT = sb("pT", [P, 2, 4, P])
        rden = sb("rden", [P, ROWS, H])
        heads = sb("heads", [P, ROWS, E])
        oT = sb("oT", [P, KE, TOK])
        x1 = sb("x1", [P, ROWS, E])
        x1_prev = sb("x1_prev", [P, ROWS, E])
        stats2 = sb("stats2", [P, ROWS, 6])
        moments2 = sb("moments2", [P, ROWS, 2])
        var_eps2 = sb("var_eps2", [P, ROWS])
        rstd2 = sb("rstd2", [P, ROWS])
        x2n = sb("x2n", [P, ROWS, E])

        wait_holder = sb("wait_holder", [P, 1])

        x2T_hi = sb("x2T_hi", [P, KE, TOK], F32R)
        x2T_lo = sb("x2T_lo", [P, KE, TOK], F32R)
        full = sb("full", [P, 4, TOK])
        y = sb("y", [P, ROWS, E])
        with nc.sbuf_tensor("wnat", [P, 2, CHUNK], F32) as wnat, \
                nc.sbuf_tensor("wstage", [P, 4, BANK], F32) as wstage, \
                nc.sbuf_tensor("wlow", [P, CHUNK], I32) as wlow:
            pass
        ha_hi = sb("ha_hi", [P, KF, TOK], F32R)
        ha_lo = sb("ha_lo", [P, KF, TOK], F32R)
        hb_hi = sb("hb_hi", [P, KF, TOK], F32R)
        hb_lo = sb("hb_lo", [P, KF, TOK], F32R)

        work = [bank("work0"), bank("work1")]
        pT_bank = bank("pT_bank")
        pv = [bank("pv0"), bank("pv1")]
        ffn = [bank("ffn0"), bank("ffn1"), bank("ffn2")]

        attn_w_in = sem("attn_w_in")
        wo_in = sem("wo_in")
        scales_in = sem("scales_in")
        gates_loaded = sem("gates_loaded")
        pool_const = sem("pool_const")
        gates_ready = sem("gates_ready")
        dve_const = sem("dve_const")
        chunk_in = [sem("chunk_in0"), sem("chunk_in1")]
        chunk_tested = sem("chunk_tested")
        low_ready = sem("low_ready")
        flag_steps = sem("flag_steps")
        wT_ready = sem("wT_ready")
        wT_copied = sem("wT_copied")
        stage_saved = [sem(f"stage_saved{i}") for i in range(4)]
        flag_sum = sem("flag_sum")
        flag_ready = sem("flag_ready")
        x_loaded = sem("x_loaded")
        c_loaded = sem("c_loaded")
        stats_ready = sem("stats_ready")
        moments_ready = sem("moments_ready")
        var_ready = sem("var_ready")
        rstd_ready = sem("rstd_ready")
        xn_ready = sem("xn_ready")
        xres_ready = sem("xres_ready")
        xT_ready, xT_copied = sem("xT_ready"), sem("xT_copied")
        cT_ready, cT_copied = sem("cT_ready"), sem("cT_copied")
        q_ready, q_copied = sem("q_ready"), sem("q_copied")
        k_ready, k_copied = sem("k_ready"), sem("k_copied")
        v_ready, v_copied = sem("v_ready"), sem("v_copied")
        kbd_ready = sem("kbd_ready")
        scores_ready = sem("scores_ready")
        masked_ready = sem("masked_ready")
        max_ready = sem("max_ready")
        probs_ready = sem("probs_ready")
        pT_ready, pT_copied = sem("pT_ready"), sem("pT_copied")
        pv_ready = sem("pv_ready")
        rden_ready = sem("rden_ready")
        heads_ready = sem("heads_ready")
        oT_ready, oT_copied = sem("oT_ready"), sem("oT_copied")
        o_ready = sem("o_ready")
        x1_ready = sem("x1_ready")
        stats2_ready = sem("stats2_ready")
        moments2_ready = sem("moments2_ready")
        var2_ready = sem("var2_ready")
        rstd2_ready = sem("rstd2_ready")
        x2n_ready = sem("x2n_ready")
        x2T_ready, x2hi_ready, x2lo_ready = sem("x2T_ready"), sem("x2hi_ready"), sem("x2lo_ready")
        x1_moved = sem("x1_moved")
        l1_ready, tanh_ready = sem("l1_ready"), sem("tanh_ready")
        silu_ready = sem("silu_ready")
        l1_full, l1_hi, l1_lo = sem("l1_full"), sem("l1_hi"), sem("l1_lo")
        l2_ready, l2_hi, l2_lo = sem("l2_ready"), sem("l2_hi"), sem("l2_lo")
        l3_ready, l3_hi, l3_lo = sem("l3_ready"), sem("l3_hi"), sem("l3_lo")
        l4_ready = sem("l4_ready")
        y_scaled, y_ready = sem("y_scaled"), sem("y_ready")
        y_stored = sem("y_stored")

        block = ctx.enter_context(nc.Block())

        def wait(eng, s, value):
            if not isinstance(value, int) or value > 0:
                eng.wait_ge(s, value)

        def quad_bank(t):
            return t % 2

        def step_bank(step):
            return WORK_STEPS.index(step) % 2

        def step_read_out(eng, n, step):
            kind, k = step
            s, per, more = {"To": (oT_copied, ROWS, k + 1), "O": (x1_ready, ROWS, k + 1),
                            "X2": (x2lo_ready, ROWS, k + 1), "x": (xT_copied, 1, 2), "c": (cT_copied, 1, 2),
                            "Q": (q_copied, 1, 2), "K": (k_copied, 1, 2), "V": (v_copied, ROWS, ROWS + k + 1)}[kind]
            wait(eng, s, per * n + more)

        def before_quad(eng, n, t):
            if t >= 2:
                wait(eng, masked_ready, NQ * n + (t - 1))
            else:
                step_read_out(eng, n - 1, WORK_STEPS[t - 2])

        def before_step(eng, n, step):
            i = WORK_STEPS.index(step)
            if isinstance(n, int) and n < 0 and i < WORK_TAIL + 2:
                return
            if i >= 2:
                step_read_out(eng, n, WORK_STEPS[i - 2])
            else:
                wait(eng, masked_ready, NQ * n + (NQ - 1 + i))

        FFN_USES = KF + 2 * PAIRS + ROWS
        assert FFN_USES % 3 == 0 and (GROUPS + 1) % 3 == 0
        L2_USE, L3_USE, L4_USE = KF, KF + PAIRS, KF + 2 * PAIRS

        def ffn_bank(u):
            return u % 3

        def before_ffn(eng, j, u):
            u -= 3
            if u < 0:
                if isinstance(j, int) and j == 0:
                    wait(eng, wT_copied, GROUPS + 1)
                    return
                j, u = j - 1, u + FFN_USES
            if u < L2_USE:
                wait(eng, l1_full, KF * j + (u + 1))
            elif u < L3_USE:
                wait(eng, l2_hi, 4 * PAIRS * j + 4 * (u - L2_USE + 1))
            elif u < L4_USE:
                wait(eng, l3_hi, 4 * PAIRS * j + 4 * (u - L3_USE + 1))
            else:
                wait(eng, y_scaled, ROWS * j + (u - L4_USE + 1))

        @block.sync
        def _(sp):
            def load(n):
                wait(sp, xn_ready, ROWS * n)
                wait(sp, xres_ready, n)
                sp.dma_start(x_in[:], x[bass.ds(n * ROWS, ROWS)].rearrange("b p e -> p b e")).then_inc(x_loaded, 16)
                wait(sp, cT_ready, n)
                sp.dma_start(c_in[:], ctx_in[bass.ds(n * ROWS, ROWS)].rearrange("b p e -> p b e"))\
                    .then_inc(c_loaded, 16)

            def store(j):
                wait(sp, y_ready, ROWS * j + ROWS)
                sp.dma_start(out[bass.ds(j * ROWS, ROWS)].rearrange("b p e -> p b e"), y[:]).then_inc(y_stored, 16)

            load(0)
            for w, t in ((Wq, wq), (Wk, wk), (Wv, wv)):
                for kt in range(KE):
                    sp.dma_start(t[:, kt, :].rearrange("p (h d) -> p h d", h=H),
                                 w[:, kt * P:(kt + 1) * P, :].rearrange("h e d -> e h d")).then_inc(attn_w_in, 16)
            for c, (src, _) in enumerate(chunks):
                if c >= 2:
                    wait(sp, wT_ready, 4 * (c - 1) + 1)
                    wait(sp, chunk_tested, c - 1)
                sp.dma_start(wnat[:, c % 2, :].rearrange("p (o e) -> p o e", o=src.shape[1]), src)\
                    .then_inc(chunk_in[c % 2], 16)
            load(1)
            with sp.Fori(1, BLOCKS - 1) as n:
                load(n + 1)
                store(n - 1)
            store(BLOCKS - 2)
            store(BLOCKS - 1)
            sp.wait_ge(y_stored, 16 * BLOCKS)

        @block.gpsimd
        def _(pool):
            pool.memset(ident[:], 0.0).then_inc(pool_const, 1)
            pool.memset(causal[:], 0.0).then_inc(pool_const, 1)
            pool.memset(headmask[:], 1.0).then_inc(pool_const, 1)
            pool.memset(minus_half[:], -0.5).then_inc(pool_const, 1)
            pool.memset(ones[:], 1.0).then_inc(pool_const, 1)
            pool.memset(v1[:], 1.0).then_inc(pool_const, 1)
            pool.wait_ge(pool_const, 6)
            pool.affine_select(out=ident[:], in_=ident[:], compare_op=ALU.not_equal, fill=1.0, base=0,
                               pattern=[[-1, P]], channel_multiplier=1).then_inc(pool_const, 1)
            pool.affine_select(out=causal[:], in_=causal[:], compare_op=ALU.is_ge, fill=MASKED, base=0,
                               pattern=[[0, 4], [-1, P]], channel_multiplier=1).then_inc(pool_const, 1)
            pool.affine_select(out=headmask[:], in_=headmask[:], compare_op=ALU.is_ge, fill=0.0, base=0,
                               pattern=[[-D, HPT]], channel_multiplier=1).then_inc(pool_const, 1)
            pool.wait_ge(pool_const, 9)
            pool.affine_select(out=headmask[:], in_=headmask[:], compare_op=ALU.is_ge, fill=0.0, base=D - 1,
                               pattern=[[D, HPT]], channel_multiplier=-1).then_inc(pool_const, 1)
            pool.wait_ge(pool_const, 10)
            pool.wait_ge(dve_const, 4)

            def make_kbd(n, i):
                if i == 0:
                    wait(pool, k_copied, n + 1)
                wait(pool, scores_ready, n * NQ + 2 * (i - KSLOTS) + 2)
                row, kt = i // KE, i % KE
                pool.tensor_tensor(kbd[:, i % KSLOTS],
                                   kT[:, kt, row * P:(row + 1) * P].unsqueeze(1).broadcast_to([P, HPT, P]),
                                   headmask[:].unsqueeze(2).broadcast_to([P, HPT, P]), ALU.mult)\
                    .then_inc(kbd_ready, 1)

            def head(n):
                wait(pool, x_loaded, 16 * n + 16)
                wait(pool, x1_ready, ROWS * n)
                pool.tensor_tensor(xres[:], x_in[:], bo_tg[:].unsqueeze(1).broadcast_to([P, ROWS, E]), ALU.add)\
                    .then_inc(xres_ready, 1)

            def head_rstd(n):
                wait(pool, var_ready, n + 1)
                pool.tensor_tensor(rstd[:], var_eps[:], minus_half[:], ALU.pow).then_inc(rstd_ready, 1)

            def body(n, ffn_on=True, attn=True, next_head=True):
                j = n - 1
                for t in range(SLOTS):
                    if attn and t in (2, 4):
                        make_kbd(n, t // 2 + 1)
                    if ffn_on and 1 <= t <= NQ:
                        m = t - 1
                        wait(pool, l1_hi, j * KF + m + 1)
                        pool.tensor_tensor(ha_lo[:, m], full[:, m % 4], ha_hi[:, m], ALU.subtract)\
                            .then_inc(l1_lo, 1)
                for kind, k in G_ORDER:
                    if kind == "N2" and attn:
                        wait(pool, var2_ready, n * ROWS + k + 1)
                        pool.tensor_tensor(rstd2[:, k:k + 1], var_eps2[:, k:k + 1], minus_half[:, 0:1], ALU.pow)\
                            .then_inc(rstd2_ready, 1)
                    if kind == "N2" and k == 0 and next_head:
                        head_rstd(n + 1)
                        head(n + 1)
                    if kind == "K" and next_head:
                        make_kbd(n + 1, 0)
                        make_kbd(n + 1, 1)

            head_rstd(0)
            head(0)
            make_kbd(0, 0)
            make_kbd(0, 1)
            body(0, ffn_on=False)
            body(1)
            with pool.Fori(2, BLOCKS - 1) as n:
                body(n)
            body(BLOCKS - 1, next_head=False)
            body(BLOCKS, attn=False, next_head=False)

        @block.vector
        def _(dve):
            dve.wait_ge(scales_in, 6 * 16)
            dve.tensor_scalar(half_s1[:], s1_col[:], 0.5, None, ALU.mult).then_inc(dve_const, 1)
            dve.wait_ge(dve_const, 1)
            dve.tensor_tensor(half_s12[:], half_s1[:], s2_col[:], ALU.mult).then_inc(dve_const, 1)
            dve.wait_ge(gates_ready, 1)
            dve.tensor_scalar(bo_tg[:], bo_tg[:], gates[:, 0:1], None, ALU.mult).then_inc(dve_const, 1)
            dve.tensor_scalar(s3_tg[:], s3_tg[:], gates[:, 1:2], None, ALU.mult).then_inc(dve_const, 1)
            dve.wait_ge(pool_const, 10)

            def hold_wait():
                dve.memset(wait_holder[:], 0.0)

            def head_stats(n):
                wait(dve, x_loaded, 16 * n + 16)
                for b in range(ROWS):
                    dve.bn_stats(stats[:, b], x_in[:, b]).then_inc(stats_ready, 1)
                wait(dve, stats_ready, ROWS * n + ROWS)
                hold_wait()
                for b in range(ROWS):
                    dve.bn_aggr(moments[:, b], stats[:, b]).then_inc(moments_ready, 1)
                wait(dve, moments_ready, ROWS * n + ROWS)
                dve.tensor_scalar(var_eps[:], moments[:, :, 1], EPS, None, ALU.add).then_inc(var_ready, 1)

            def head_norm(n):
                wait(dve, rstd_ready, n + 1)
                wait(dve, xT_ready, n)
                for b in range(ROWS):
                    dve.tensor_scalar(xn[:, b], x_in[:, b], moments[:, b, 0:1], rstd[:, b:b + 1],
                                      ALU.subtract, ALU.mult).then_inc(xn_ready, 1)

            def keys(n):
                use = step_bank(("K", 0))
                wait(dve, k_ready, n + 1)
                wait(dve, kbd_ready, 2 * ROWS * n)
                dve.tensor_copy(kT[:], work[use][:].rearrange("p (m t) -> p m t", m=KE))\
                    .then_inc(k_copied, 1)

            def values(n, b):
                use = step_bank(("V", b))
                wait(dve, v_ready, ROWS * n + b + 1)
                wait(dve, pv_ready, NQ * n)
                dve.tensor_copy(v1[:, b, :, 0:D], work[use][:, 0:E].rearrange("p (h d) -> p h d", h=H))\
                    .then_inc(v_copied, 1)

            def mask_and_max(n, t):
                use = quad_bank(t)
                slot = t % PSLOTS
                wait(dve, scores_ready, n * NQ + t + 1)
                wait(dve, pT_ready, n * NQ + (t - PSLOTS + 1))
                dve.scalar_tensor_tensor(probs[:, slot], work[use][:].rearrange("p (h t) -> p h t", h=4), SCALE,
                                         causal[:], ALU.mult, ALU.add)\
                    .then_inc(masked_ready, 1)
                wait(dve, masked_ready, n * NQ + t + 1)
                dve.tensor_reduce(negmax[:, slot], probs[:, slot], AX_X, ALU.max, negate=True).then_inc(max_ready, 1)

            def normalise(n, b):
                o = pv[b][:, 0:H * (D + 1)].rearrange("p (h d) -> p h d", h=H)
                wait(dve, pv_ready, n * NQ + (b + 1) * QROW)
                dve.reciprocal(rden[:, b], o[:, :, D]).then_inc(rden_ready, 1)
                wait(dve, rden_ready, n * ROWS + b + 1)
                wait(dve, oT_ready, (n - 1) * ROWS + b + 1)
                dve.tensor_tensor(heads[:, b].rearrange("p (h d) -> p h d", h=H), o[:, :, 0:D],
                                  rden[:, b].unsqueeze(2).broadcast_to([P, H, D]), ALU.mult)\
                    .then_inc(heads_ready, 1)

            def l1_gate(j, m):
                use = ffn_bank(m)
                u, v = ffn[use][:, 0:TOK], ffn[use][:, TOK:2 * TOK]
                f = full[:, m % 4]
                wait(dve, tanh_ready, j * KF + m + 1)
                dve.scalar_tensor_tensor(f, f, 1.0, u, ALU.add, ALU.mult).then_inc(silu_ready, 1)
                wait(dve, silu_ready, j * KF + m + 1)
                dve.scalar_tensor_tensor(f, v, half_s12[:, m:m + 1], f, ALU.mult, ALU.mult)\
                    .then_inc(l1_full, 1)
                wait(dve, l1_full, j * KF + m + 1)
                wait(dve, l4_ready, ROWS * j)
                dve.tensor_copy(ha_hi[:, m], f).then_inc(l1_hi, 1)

            def lows(j, p, hi_sem, hi, lo, lo_sem):
                wait(dve, hi_sem, (j * PAIRS + p + 1) * 4)
                f = full[:, 2 * (p % 2):2 * (p % 2) + 2]
                dve.tensor_tensor(lo[:, 2 * p:2 * p + 2], f, hi[:, 2 * p:2 * p + 2], ALU.subtract)\
                    .then_inc(lo_sem, 1)

            def body(n, ffn_on=True, attn=True, next_head=True, weights=False):
                j = n - 1
                for t in range(SLOTS):
                    if attn and t < NQ:
                        mask_and_max(n, t)
                    if ffn_on and 1 <= t <= NQ:
                        l1_gate(j, t - 1)
                    if attn and t == QROW + 3:
                        normalise(n, 0)
                    if ffn_on and t == NQ + 1:
                        wait(dve, y_ready, ROWS * j)
                        wait(dve, x2n_ready, ROWS * j + ROWS)
                        dve.tensor_copy(x1_prev[:], x1[:]).then_inc(x1_moved, 1)
                    if weights:
                        dve.wait_ge(chunk_in[t % 2], 16 * (t // 2 + 1))
                        wait(dve, chunk_tested, t)
                        dve.tensor_scalar(wlow[:], wnat[:, t % 2].bitcast(I32), LOW_BITS, None, ALU.bitwise_and)\
                            .then_inc(low_ready, 1)
                        dve.wait_ge(low_ready, t + 1)
                        dve.tensor_reduce(low_max[:, t:t + 1], wlow[:], AX_X, ALU.max).then_inc(chunk_tested, 1)
                if attn:
                    normalise(n, 1)
                if weights:
                    dve.wait_ge(chunk_tested, CHUNKS)
                    dve.tensor_reduce(low_all[:], low_max[:], AX_X, ALU.max).then_inc(flag_steps, 1)
                    dve.wait_ge(flag_steps, 1)
                    dve.tensor_scalar(inexact[:], low_all[:], 1.0, None, ALU.min).then_inc(flag_steps, 1)
                if next_head:
                    head_stats(n + 1)
                for kind, k in G_ORDER:
                    if kind == "L2" and ffn_on:
                        lows(j, k, l2_hi, hb_hi, hb_lo, l2_lo)
                    if kind == "L3" and ffn_on:
                        lows(j, k, l3_hi, ha_hi, ha_lo, l3_lo)
                    if kind == "L4" and ffn_on:
                        use = ffn_bank(L4_USE + k)
                        wait(dve, l4_ready, ROWS * j + k + 1)
                        wait(dve, y_stored, 16 * j)
                        dve.tensor_tensor(y[:, k], ffn[use][:, 0:E], s3_tg[:], ALU.mult)\
                            .then_inc(y_scaled, 1)
                        wait(dve, y_scaled, ROWS * j + k + 1)
                        dve.tensor_tensor(y[:, k], y[:, k], x1_prev[:, k], ALU.add).then_inc(y_ready, 1)
                    if kind == "O" and attn:
                        use = step_bank((kind, k))
                        wait(dve, o_ready, n * ROWS + k + 1)
                        wait(dve, xres_ready, n + 1)
                        wait(dve, x1_moved, n)
                        dve.scalar_tensor_tensor(x1[:, k], work[use][:, 0:E], gates[:, 0:1], xres[:, k],
                                                 ALU.mult, ALU.add).then_inc(x1_ready, 1)
                        wait(dve, x1_ready, n * ROWS + k + 1)
                        dve.bn_stats(stats2[:, k], x1[:, k]).then_inc(stats2_ready, 1)
                        wait(dve, stats2_ready, n * ROWS + k + 1)
                        hold_wait()
                        dve.bn_aggr(moments2[:, k], stats2[:, k]).then_inc(moments2_ready, 1)
                        wait(dve, moments2_ready, n * ROWS + k + 1)
                        dve.tensor_scalar(var_eps2[:, k:k + 1], moments2[:, k, 1:2], EPS, None, ALU.add)\
                            .then_inc(var2_ready, 1)
                    if kind == "N2" and attn:
                        wait(dve, rstd2_ready, n * ROWS + k + 1)
                        wait(dve, x2T_ready, (n - 1) * ROWS + k + 1)
                        dve.tensor_scalar(x2n[:, k], x1[:, k], moments2[:, k, 0:1], rstd2[:, k:k + 1],
                                          ALU.subtract, ALU.mult).then_inc(x2n_ready, 1)
                        if k == 1 and next_head:
                            head_norm(n + 1)
                    if kind == "X2" and attn:
                        use = step_bank((kind, k))
                        wait(dve, x2hi_ready, n * ROWS + k + 1)
                        dve.tensor_tensor(x2T_lo[:, :, k * P:(k + 1) * P],
                                          work[use][:, 0:E].rearrange("p (m t) -> p m t", m=KE),
                                          x2T_hi[:, :, k * P:(k + 1) * P], ALU.subtract)\
                            .then_inc(x2lo_ready, 1)
                    if kind == "K" and next_head:
                        keys(n + 1)
                    if kind == "V" and next_head:
                        values(n + 1, k)

            head_stats(0)
            head_norm(0)
            keys(0)
            for b in range(ROWS):
                values(0, b)
            body(0, ffn_on=False, weights=True)
            dve.wait_ge(flag_sum, 1)
            dve.tensor_copy(flag[:], pT_bank[0:1, 0:1]).then_inc(flag_ready, 1)
            body(1)
            with dve.Fori(2, BLOCKS - 1) as n:
                body(n)
            body(BLOCKS - 1, next_head=False)
            body(BLOCKS, attn=False, next_head=False)

        @block.scalar
        def _(act):
            act.dma_start(gates_in[:, 0:1], g_xattn.rearrange("(a n) -> a n", a=1).partition_broadcast(P))\
                .then_inc(gates_loaded, 16)
            act.dma_start(gates_in[:, 1:2], g_ffn.rearrange("(a n) -> a n", a=1).partition_broadcast(P))\
                .then_inc(gates_loaded, 16)
            act.dma_start(bo_tg[:], bo.rearrange("(a n) -> a n", a=1).partition_broadcast(P))\
                .then_inc(scales_in, 16)
            act.dma_start(s3_tg[:], w3s.rearrange("(a n) -> a n", a=1).partition_broadcast(P))\
                .then_inc(scales_in, 16)
            for s, t in ((s1, s1_col), (s2, s2_col), (h1s, h1s_col), (h2s, h2s_col)):
                act.dma_start(t[:], s.rearrange("(m p) -> p m", p=P), allow_slow_non_contiguous=True).then_inc(scales_in, 16)
            act.dma_start(wo_nat[:], Wo.rearrange("(o p) e -> p o e", p=P)).then_inc(wo_in, 16)
            act.wait_ge(gates_loaded, 32)
            act.activation(gates[:], gates_in[:], ACT.Tanh).then_inc(gates_ready, 1)
            act.wait_ge(scales_in, 6 * 16)

            def copy_wT(g):
                act.wait_ge(wT_ready, g + 1)
                if g == 0:
                    dst = woT[:].rearrange("p k e -> p (k e)")
                else:
                    s = (g - 1) % 4
                    if g > 4:
                        act.wait_ge(stage_saved[s], 16 * ((g - 1) // 4))
                    dst = wstage[:, s]
                act.activation(dst, ffn[g % 3][:], ACT.Copy).then_inc(wT_copied, 1)

            def save_wT(g):
                _, _, at = groups[g - 1]
                act.wait_ge(wT_copied, g + 1)
                act.dma_start(W[:, at:at + BANK].bitcast(F32), wstage[:, (g - 1) % 4])\
                    .then_inc(stage_saved[(g - 1) % 4], 16)

            def head_step(n, kind):
                use = step_bank((kind, 0))
                src = work[use][:].rearrange("p (m t) -> p m t", m=KE)
                if kind == "x":
                    wait(act, xT_ready, n + 1)
                    wait(act, q_ready, n)
                    act.activation(xT[:], src, ACT.Copy).then_inc(xT_copied, 1)
                if kind == "c":
                    wait(act, cT_ready, n + 1)
                    wait(act, v_ready, ROWS * n)
                    act.activation(cT[:], src, ACT.Copy).then_inc(cT_copied, 1)
                if kind == "Q":
                    wait(act, q_ready, n + 1)
                    wait(act, scores_ready, NQ * n)
                    act.activation(qT[:], src, ACT.Copy).then_inc(q_copied, 1)

            def exps(n, t):
                slot = t % PSLOTS
                wait(act, max_ready, n * NQ + t + 1)
                for h in range(4):
                    last = act.activation(probs[:, slot, h], probs[:, slot, h], ACT.Exp,
                                          bias=negmax[:, slot, h:h + 1])
                last.then_inc(probs_ready, 1)

            def copy_pT(n, t):
                wait(act, pT_ready, n * NQ + t + 1)
                wait(act, pv_ready, n * NQ + (t - 1))
                act.activation(pT[:, t % 2], pT_bank[:].rearrange("p (h t) -> p h t", h=4), ACT.Copy)\
                    .then_inc(pT_copied, 1)

            def gelus(j, p, first_use, ready, scales, hi, hi_sem):
                use = ffn_bank(first_use + p)
                wait(act, ready, j * PAIRS + p + 1)
                for r in range(2):
                    m = 2 * p + r
                    src = ffn[use][:, r * TOK:(r + 1) * TOK]
                    act.activation(full[:, 2 * (p % 2) + r], src, ACT.Gelu, scale=scales[:, m:m + 1])\
                        .then_inc(hi_sem, 1)
                    act.activation(hi[:, m], src, ACT.Gelu, scale=scales[:, m:m + 1]).then_inc(hi_sem, 1)

            def body(n, ffn_on=True, attn=True, next_head=True, weights=False):
                j = n - 1
                for t in range(SLOTS):
                    if attn and 1 <= t <= NQ:
                        exps(n, t - 1)
                    if ffn_on and t < NQ:
                        use = ffn_bank(t)
                        wait(act, l1_ready, j * KF + t + 1)
                        wait(act, l3_lo, PAIRS * j)
                        if t >= 4:
                            wait(act, l1_lo, j * KF + (t - 3))
                        act.activation(full[:, t % 4], ffn[use][:, 0:TOK], ACT.Tanh, scale=half_s1[:, t:t + 1])\
                            .then_inc(tanh_ready, 1)
                    if attn and 2 <= t <= NQ + 1:
                        copy_pT(n, t - 2)
                    if weights:
                        for g in range(4 * t + 1, 4 * t + 5):
                            copy_wT(g)
                            if g > 1:
                                save_wT(g - 1)
                if weights:
                    save_wT(GROUPS)
                for kind, k in G_ORDER:
                    if kind == "L2" and ffn_on:
                        if k < 2:
                            wait(act, l1_lo, j * KF + KF)
                        else:
                            wait(act, l2_lo, j * PAIRS + (k - 1))
                        wait(act, l3_ready, j * PAIRS)
                        gelus(j, k, L2_USE, l2_ready, h1s_col, hb_hi, l2_hi)
                    if kind == "L3" and ffn_on:
                        if k < 2:
                            wait(act, l2_lo, j * PAIRS + (PAIRS - 1 + k))
                        else:
                            wait(act, l3_lo, j * PAIRS + (k - 1))
                        wait(act, l2_ready, j * PAIRS + PAIRS)
                        gelus(j, k, L3_USE, l3_ready, h2s_col, ha_hi, l3_hi)
                    if kind == "To" and attn:
                        use = step_bank((kind, k))
                        wait(act, oT_ready, n * ROWS + k + 1)
                        wait(act, o_ready, (n - 1) * ROWS + k + 1)
                        act.activation(oT[:, :, k * P:(k + 1) * P],
                                       work[use][:, 0:E].rearrange("p (m t) -> p m t", m=KE), ACT.Copy)\
                            .then_inc(oT_copied, 1)
                    if kind == "X2" and attn:
                        use = step_bank((kind, k))
                        wait(act, x2T_ready, n * ROWS + k + 1)
                        wait(act, l1_ready, KF * n)
                        act.activation(x2T_hi[:, :, k * P:(k + 1) * P],
                                       work[use][:, 0:E].rearrange("p (m t) -> p m t", m=KE), ACT.Copy)\
                            .then_inc(x2hi_ready, 1)
                    if kind in ("x", "c", "Q") and next_head:
                        head_step(n + 1, kind)

            copy_wT(0)
            for kind in ("x", "c", "Q"):
                head_step(0, kind)
            body(0, ffn_on=False, weights=True)
            body(1)
            with act.Fori(2, BLOCKS - 1) as n:
                body(n)
            body(BLOCKS - 1, next_head=False)
            body(BLOCKS, attn=False, next_head=False)

        @block.tensor
        def _(pe):
            def transpose_w(g):
                wait(pe, wT_copied, g - 2)
                if g == 0:
                    pe.wait_ge(wo_in, 16)
                    tiles = [wo_nat[:, o, kt * P:(kt + 1) * P] for kt in range(KE) for o in range(KE)]
                else:
                    c, where, _ = groups[g - 1]
                    pe.wait_ge(chunk_in[c % 2], 16 * (c // 2 + 1))
                    width = chunks[c][0].shape[2]
                    nat = wnat[:, c % 2, :].rearrange("p (o e) -> p o e", e=width)
                    tiles = [nat[:, o, e:e + P] for o, e in where]
                for i, tile in enumerate(tiles):
                    last = pe.transpose(ffn[g % 3][:, i * P:(i + 1) * P], tile, ident[:])
                last.then_inc(wT_ready, 1)

            def project(dst, lhsT, rhs):
                for kt in range(KE):
                    last = pe.matmul(dst, lhsT(kt), rhs(kt), start=kt == 0, stop=kt == KE - 1)
                return last

            def head_step(n, step):
                kind, k = step
                bank_ = work[step_bank(step)]
                before_step(pe, n - 1, step)
                if kind == "x":
                    wait(pe, xn_ready, ROWS * n + ROWS)
                    for kt in range(KE):
                        for b in range(ROWS):
                            last = pe.transpose(bank_[:, (kt * ROWS + b) * P:(kt * ROWS + b + 1) * P],
                                                xn[:, b, kt * P:(kt + 1) * P], ident[:])
                    last.then_inc(xT_ready, 1)
                if kind == "c":
                    wait(pe, c_loaded, 16 * n + 16)
                    for kt in range(KE):
                        for b in range(ROWS):
                            last = pe.transpose(bank_[:, (kt * ROWS + b) * P:(kt * ROWS + b + 1) * P],
                                                c_in[:, b, kt * P:(kt + 1) * P], ident[:])
                    last.then_inc(cT_ready, 1)
                if kind in ("Q", "K"):
                    w, src = (wq, xT) if kind == "Q" else (wk, cT)
                    wait(pe, xT_copied if kind == "Q" else cT_copied, n + 1)
                    for m in range(KE):
                        last = project(bank_[:, m * TOK:(m + 1) * TOK], lambda kt: w[:, kt, m * P:(m + 1) * P],
                                       lambda kt: src[:, kt])
                    last.then_inc(q_ready if kind == "Q" else k_ready, 1)
                if kind == "V":
                    project(bank_[:, 0:E], lambda kt: cT[:, kt, k * P:(k + 1) * P], lambda kt: wv[:, kt])\
                        .then_inc(v_ready, 1)

            def scores(n, t):
                use = quad_bank(t)
                row, q = t // QROW, t % QROW
                before_quad(pe, n, t)
                if t == 0:
                    wait(pe, q_copied, n + 1)
                wait(pe, kbd_ready, n * 2 * ROWS + (t // 2 + 1))
                pe.matmul(work[use][:], qT[:, q // 2, row * P:(row + 1) * P],
                          kbd[:, (t // 2) % KSLOTS, 4 * (q % 2):4 * (q % 2) + 4], start=True, stop=True)\
                    .then_inc(scores_ready, 1)

            def transpose_probs(n, t):
                wait(pe, probs_ready, n * NQ + t + 1)
                wait(pe, pT_copied, n * NQ + t)
                for h in range(4):
                    last = pe.transpose(pT_bank[:, h * P:(h + 1) * P], probs[:, t % PSLOTS, h], ident[:])
                last.then_inc(pT_ready, 1)

            def probs_values(n, t):
                row, q = t // QROW, t % QROW
                wait(pe, pT_copied, n * NQ + t + 1)
                if q == 0:
                    wait(pe, v_copied, n * ROWS + row + 1)
                    wait(pe, heads_ready, (n - 1) * ROWS + row + 1)
                for i in range(4):
                    h = 4 * q + i
                    last = pe.matmul(pv[row][:, h * (D + 1):(h + 1) * (D + 1)], pT[:, t % 2, i], v1[:, row, h],
                                     start=True, stop=True)
                last.then_inc(pv_ready, 1)

            def run(general, first):
                def mm(dst, w, h, **flags):
                    if general:
                        w, h = w.bitcast(F32), h.bitcast(F32)
                    return pe.matmul(dst, w, h, **flags)

                def hidden(dst, weight_at, tiles, m, his, los, out_width):
                    n_mm = 2 * tiles
                    i = 0
                    for kt in range(tiles):
                        for part in (his, los):
                            at = weight_at + kt * out_width + m * P
                            last = mm(dst, W[:, at:at + P], part[:, kt], start=i == 0, stop=i == n_mm - 1)
                            i += 1
                    return last

                def body(n, ffn_on=True, attn=True, next_head=True, weights=False):
                    j = n - 1
                    for t in range(SLOTS):
                        if ffn_on and t < NQ:
                            use = ffn_bank(t)
                            before_ffn(pe, j, t)
                            if t == 0:
                                wait(pe, x2lo_ready, ROWS * j + ROWS)
                            hidden(ffn[use][:, 0:TOK], W1_AT, KE, t, x2T_hi, x2T_lo, F)
                            hidden(ffn[use][:, TOK:2 * TOK], W2_AT, KE, t, x2T_hi, x2T_lo, F).then_inc(l1_ready, 1)
                        if attn and t < NQ:
                            scores(n, t)
                        if attn and 2 <= t <= NQ + 1:
                            transpose_probs(n, t - 2)
                        if attn and t >= 3:
                            probs_values(n, t - 3)
                        if weights:
                            for g in range(4 * t + 1, 4 * t + 5):
                                transpose_w(g)
                    if weights:
                        pe.wait_ge(flag_steps, 2)
                        pe.wait_ge(pT_copied, NQ)
                        pe.matmul(pT_bank[0:1, 0:1], inexact[:], ones[:], start=True, stop=True).then_inc(flag_sum, 1)
                    for step in G_ORDER:
                        kind, k = step
                        if kind == "L2" and ffn_on:
                            use = ffn_bank(L2_USE + k)
                            before_ffn(pe, j, L2_USE + k)
                            if k == 0:
                                wait(pe, l1_hi, KF * j + KF)
                                wait(pe, l1_lo, KF * j + KF)
                            for r in range(2):
                                last = hidden(ffn[use][:, r * TOK:(r + 1) * TOK], H1_AT, KF, 2 * k + r,
                                              ha_hi, ha_lo, F)
                            last.then_inc(l2_ready, 1)
                        if kind == "L3" and ffn_on:
                            use = ffn_bank(L3_USE + k)
                            before_ffn(pe, j, L3_USE + k)
                            if k == 0:
                                wait(pe, l2_lo, PAIRS * j + PAIRS)
                            for r in range(2):
                                last = hidden(ffn[use][:, r * TOK:(r + 1) * TOK], H2_AT, KF, 2 * k + r,
                                              hb_hi, hb_lo, F)
                            last.then_inc(l3_ready, 1)
                        if kind == "L4" and ffn_on:
                            use = ffn_bank(L4_USE + k)
                            before_ffn(pe, j, L4_USE + k)
                            if k == 0:
                                wait(pe, l3_lo, PAIRS * j + PAIRS)
                            for kt in range(KF):
                                for i, part in enumerate((ha_hi, ha_lo)):
                                    last = mm(ffn[use][:, 0:E], part[:, kt, k * P:(k + 1) * P],
                                              W[:, W3_AT + kt * E:W3_AT + (kt + 1) * E],
                                              start=kt == 0 and i == 0, stop=kt == KF - 1 and i == 1)
                            last.then_inc(l4_ready, 1)
                        if kind in ("To", "O", "X2") and attn:
                            use = step_bank(step)
                            before_step(pe, n, step)
                            if kind == "O":
                                wait(pe, oT_copied, n * ROWS + k + 1)
                                project(work[use][:, 0:E], lambda kt: oT[:, kt, k * P:(k + 1) * P],
                                        lambda kt: woT[:, kt]).then_inc(o_ready, 1)
                            else:
                                src, ready, done = (heads, heads_ready, oT_ready) if kind == "To" else \
                                    (x2n, x2n_ready, x2T_ready)
                                wait(pe, ready, n * ROWS + k + 1)
                                for kt in range(KE):
                                    last = pe.transpose(work[use][:, kt * P:(kt + 1) * P],
                                                        src[:, k, kt * P:(kt + 1) * P], ident[:])
                                last.then_inc(done, 1)
                        if kind in HEAD_KINDS and next_head:
                            head_step(n + 1, step)

                if first == 0:
                    body(0, ffn_on=False, weights=True)
                    return
                body(1)
                with pe.Fori(2, BLOCKS - 1) as n:
                    body(n)
                body(BLOCKS - 1, next_head=False)
                body(BLOCKS, attn=False, next_head=False)

            pe.wait_ge(pool_const, 10)
            transpose_w(0)
            for step in HEAD_STEPS:
                if step[0] == "Q":
                    pe.wait_ge(attn_w_in, 3 * KE * 16)
                head_step(0, step)
            run(False, 0)
            pe.wait_ge(flag_ready, 1)
            for s in stage_saved:
                pe.wait_ge(s, 16 * (GROUPS // 4))
            any_inexact = pe.value_load(flag[0:1, 0:1])
            with pe.If(any_inexact > 0):
                run(True, 1)
            with pe.Else():
                run(False, 1)


_INS = ["x", "ctx_1024", "g_xattn", "g_ffn", "L0_xattn_Wq", "L0_xattn_Wk", "L0_xattn_Wv", "L0_xattn_Wo",
        "L0_xattn_bo", "L0_ffn_w1_w", "L0_ffn_w1_s", "L0_ffn_w2_w", "L0_ffn_w2_s", "L0_ffn_h1_w", "L0_ffn_h1_s",
        "L0_ffn_h2_w", "L0_ffn_h2_s", "L0_ffn_w3_w", "L0_ffn_w3_s"]


def kernel(**inputs):
    import numpy as np
    import concourse.bacc as bacc
    from concourse.bass_utils import run_bass_kernel_spmd

    nc = bacc.Bacc("TRN2", target_bir_lowering=False, num_devices=1)
    arrays, args = {}, []
    for name in _INS:
        a = np.ascontiguousarray(inputs[name])
        arrays[f"in_{name}"] = a
        args.append(nc.dram_tensor(f"in_{name}", a.shape, mybir.dt.from_np(a.dtype), kind="ExternalInput").ap())
    shape = arrays["in_x"].shape
    args.append(nc.dram_tensor("out", shape, F32, kind="ExternalOutput").ap())
    program(nc, *args)
    result = run_bass_kernel_spmd(nc, [arrays], core_ids=[0])
    return result.results[0]["out"]
```

```python
from contextlib import ExitStack

import concourse.bass as bass
from concourse import mybir

ALU = mybir.AluOpType
ACT = mybir.ActivationFunctionType
F32 = mybir.dt.float32
F32R = mybir.dt.float32r
I32 = mybir.dt.int32
F16 = mybir.dt.float16
BF16 = mybir.dt.bfloat16
AX_X = mybir.AxisListType.X

P = 128
ROWS = 2
TOK = ROWS * P
BANK = 512
LOW_BITS = 0xFFF
MASKED = -1e9
EPS = 1e-5

ORDER = [(step.rstrip("+").split(".")[0], int((step.rstrip("+") + ".0").split(".")[1]), int(step[-1] == "+"))
         for step in """
    L1.0 a1.0 L1.1 T.0 a1.1 g.0 f.0 t.0 h.0 g.1 W.0 u.0 e.1 l.0 S.2 W.1 s.2 f.1 L1.2 m.2 PV.0 a1.2 W.2 h.1 T.1
    t.1 l.1 W.3 g.2 u.1 f.2 L1.3 e.2 S.3 a1.3 h.2 L1.4 kb.4 l.2 PV.1 s.3 W.4 a1.4 g.3 f.3 T.2 h.3 l.3 L1.5 t.2
    m.3 u.2 g.4 e.3 f.4 a1.5 h.4 L1.6 g.5 f.5 a1.6 h.5 L1.7 g.6 f.6 l.4 PV.2 l.5 a1.7 h.6 T.3 g.7 t.3 f.7 W.5
    h.7 l.6 u.3 W.6 a2.0 L2.0 PV.3 nh.0 l.7 nh.1 a2.1 kb.5 to.0 nm.0 nm.1 mv st+ L2.1 To.0 L2.2 L2.3 a2.2 a2.3
    W.7 w2.0 W.8 o.0 n2.0 O.0 kb.6 L2.4 W.9 nx+ L2.5 x2.0 X2.0 a2.4 a2.5 w2.1 X+ L2.6 S.4 w2.2 s.4 m.4 x+ a2.6
    L2.7 S.5 s.5 a2.7 w2.3 m.5 S.6 e.4 e.5 W.10 L3.0 C+ T.4 t.4 u.4 L3.1 s.6 PV.4 c+ T.5 t.5 m.6 e.6 kb.7 u.5
    S.7 s.7 L3.2 m.7 T.6 PV.5 t.6 u.6 Q+ nh.2 L3.3 nm.2 e.7 q+ T.7 t.7 K+ u.7 k+ a3.0 nh.3 nm.3 a3.1 kb.0+ L3.4
    PV.6 v.0+ PV.7 v.1+ V.0+ to.1 w3.0 V.1+ L3.5 To.1 L3.6 a3.2 a3.3 w3.1 o.1 a3.4 O.1 w3.2 kb.1+ n2.1 L3.7 w3.3
    a3.5 S.0+ L4.0 s.0+ S.1+ rx+ kb.2+ a3.6 a3.7 m.0+ L4.1 X2.1 x2.1 L4.2 kb.3+ s.1+ y.0 y.1 L4.3 z.0 z.1 m.1+
    e.0+
""".split()]
ATTN_WORK = ("S", "To", "O", "X2")
HEAD_WORK = ("X", "C", "Q", "K", "V")
WORK_STEPS = [s for s in ORDER if s[0] in ATTN_WORK + HEAD_WORK]
assert len(WORK_STEPS) % 2 == 0


def program(nc, x, ctx_in, g_xattn, g_ffn, Wq, Wk, Wv, Wo, bo, w1, s1, w2, s2, h1, h1s, h2, h2s, w3, w3s, out):
    B, S, E = x.shape
    H, _, D = Wq.shape
    F = w1.shape[0]
    BLOCKS = B // ROWS
    KE = E // P
    KF = F // P
    NQ = ROWS * H // 4
    QROW = H // 4
    HPT = P // D
    SCALE = 1.0 / float(D) ** 0.5
    PAIRS = KF // 2
    assert S == P and H * D == E and KE == 2 and KF == NQ == 8 and QROW == 2 * KE

    W1_AT, W2_AT, H1_AT = 0, KE * F, 2 * KE * F
    H2_AT, W3_AT = H1_AT + KF * F, H1_AT + 2 * KF * F
    W_COLS = W3_AT + KF * E

    CHUNK = 4 * BANK
    chunks = []
    for w, at in ((w1, W1_AT), (w2, W2_AT)):
        chunks.append((w.rearrange("(o p) e -> p o e", p=P),
                       [([(4 * q + r, kt * P) for r in range(4)], at + kt * F + 4 * q * P)
                        for q in range(2) for kt in range(KE)]))
    for w, at in ((h1, H1_AT), (h2, H2_AT)):
        for q in range(2):
            for c in range(2):
                src = w[q * BANK:(q + 1) * BANK, c * BANK:(c + 1) * BANK].rearrange("(o p) e -> p o e", p=P)
                chunks.append((src, [([(r, k * P) for r in range(4)], at + (4 * c + k) * F + 4 * q * P)
                                     for k in range(4)]))
    chunks.append((w3.rearrange("(o p) e -> p o e", p=P),
                   [([(0, kt * P), (1, kt * P), (0, (kt + 1) * P), (1, (kt + 1) * P)], W3_AT + kt * E)
                    for kt in range(0, KF, 2)]))
    CHUNKS = len(chunks)
    groups = [(c, tiles, at) for c, (_, gs) in enumerate(chunks) for tiles, at in gs]
    GROUPS = len(groups)
    assert CHUNKS == sum(step[0] == "W" for step in ORDER)
    PARTS = 3
    VCOLS = PARTS * D + 1
    HALF = P // 2
    PT_SCALE = 32768.0
    PAIR = 8

    with ExitStack() as ctx:
        def sb(name, shape, dt=F32):
            return ctx.enter_context(nc.sbuf_tensor(name, shape, dt))

        def bank(name):
            return ctx.enter_context(nc.psum_tensor(name, [P, BANK], F32))

        def sem(name):
            return ctx.enter_context(nc.semaphore(name))

        W = sb("W", [P, W_COLS], F32R)
        wq = sb("wq", [P, KE, E])
        wk = sb("wk", [P, KE, E])
        wv = sb("wv", [P, KE, E])
        wo_nat = sb("wo_nat", [P, KE, E])
        woT = sb("woT", [P, KE, E])
        ident = sb("ident", [P, P])
        causal = sb("causal", [P, 4, P])
        headmask = sb("headmask", [P, HPT])
        quadmask = sb("quadmask", [P, 4])
        bo_tg = sb("bo_tg", [P, E])
        s3_tg = sb("s3_tg", [P, E])
        gates_in = sb("gates_in", [P, 2])
        gates = sb("gates", [P, 2])
        s1_col = sb("s1_col", [P, KF])
        s2_col = sb("s2_col", [P, KF])
        half_s1 = sb("half_s1", [P, KF])
        half_s12 = sb("half_s12", [P, KF])
        h1s_col = sb("h1s_col", [P, KF])
        h2s_col = sb("h2s_col", [P, KF])
        minus_half = sb("minus_half", [P, ROWS])
        ones = sb("ones", [P, 1])
        low_all = sb("low_all", [P, 1], I32)
        inexact = sb("inexact", [P, 1])
        flag = sb("flag", [1, 1], I32)

        x_in = sb("x_in", [P, ROWS, E])
        c_in = sb("c_in", [P, ROWS, E])
        stats = sb("stats", [P, ROWS, 6])
        moments = sb("moments", [P, ROWS, 2])
        var_eps = sb("var_eps", [P, ROWS])
        rstd = sb("rstd", [P, ROWS])
        xn = sb("xn", [P, ROWS, E])
        xres = sb("xres", [P, ROWS, E])
        xT = sb("xT", [P, KE, TOK])
        cT = sb("cT", [P, KE, TOK])
        qs = sb("qs", [P, 2, KE, TOK], F32R)
        k_lo = sb("k_lo", [P, 2, KE, TOK])
        k_hi = sb("k_hi", [P, 2, KE, TOK], F32R)
        KSLOTS = 2
        kbd = sb("kbd", [P, KSLOTS, 2, 4, P], F32R)
        vs = sb("vs", [P, ROWS, H, VCOLS], BF16)
        v_rest = sb("v_rest", [P, ROWS, E])
        PSLOTS = 4
        probs = sb("probs", [P, PSLOTS, 4, P])
        negmax = sb("negmax", [P, PSLOTS, 4])
        pT_hi = sb("pT_hi", [P, 2, 4, P], F16)
        pT_lo = sb("pT_lo", [P, 2, 4, P], F16)
        head_sum = sb("head_sum", [P, 2, PAIR, D])
        rden = sb("rden", [P, ROWS, H])
        heads = sb("heads", [P, ROWS, E])
        oT = sb("oT", [P, KE, TOK])
        x1 = sb("x1", [P, ROWS, E])
        x1_prev = sb("x1_prev", [P, ROWS, E])
        stats2 = sb("stats2", [P, ROWS, 6])
        moments2 = sb("moments2", [P, ROWS, 2])
        var_eps2 = sb("var_eps2", [P, ROWS])
        rstd2 = sb("rstd2", [P, ROWS])
        x2n = sb("x2n", [P, ROWS, E])

        wait_holder = sb("wait_holder", [P, 1])

        x2T_hi = sb("x2T_hi", [P, KE, TOK], F32R)
        x2T_lo = sb("x2T_lo", [P, KE, TOK], F32R)
        full = sb("full", [P, 4, TOK])
        y = sb("y", [P, ROWS, E])
        with nc.sbuf_tensor("wnat", [P, 2, CHUNK], F32) as wnat, \
                nc.sbuf_tensor("wstage", [P, 4, BANK], F32) as wstage, \
                nc.sbuf_tensor("wlow", [P, CHUNK], I32) as wlow:
            pass
        ha_hi = sb("ha_hi", [P, KF, TOK], F32R)
        ha_lo = sb("ha_lo", [P, KF, TOK], F32R)
        hb_hi = sb("hb_hi", [P, KF, TOK], F32R)
        hb_lo = sb("hb_lo", [P, KF, TOK], F32R)

        work = [bank("work0"), bank("work1")]
        pT_bank = bank("pT_bank")
        pv = [bank("pv0"), bank("pv1")]
        ffn = [bank("ffn0"), bank("ffn1"), bank("ffn2")]

        attn_w_in = sem("attn_w_in")
        wo_in = sem("wo_in")
        scales_in = sem("scales_in")
        gates_loaded = sem("gates_loaded")
        pool_const = sem("pool_const")
        gates_ready = sem("gates_ready")
        dve_const = sem("dve_const")
        chunk_in = [sem("chunk_in0"), sem("chunk_in1")]
        chunk_tested = sem("chunk_tested")
        flag_steps = sem("flag_steps")
        wT_ready = sem("wT_ready")
        wT_copied = sem("wT_copied")
        stage_saved = [sem(f"stage_saved{i}") for i in range(4)]
        flag_sum = sem("flag_sum")
        flag_ready = sem("flag_ready")
        x_loaded = sem("x_loaded")
        c_loaded = sem("c_loaded")
        stats_ready = sem("stats_ready")
        moments_ready = sem("moments_ready")
        var_ready = sem("var_ready")
        rstd_ready = sem("rstd_ready")
        xn_ready = sem("xn_ready")
        xres_ready = sem("xres_ready")
        xT_ready, xT_copied = sem("xT_ready"), sem("xT_copied")
        cT_ready, cT_copied = sem("cT_ready"), sem("cT_copied")
        q_ready, q_hi_ready, q_lo_ready = sem("q_ready"), sem("q_hi_ready"), sem("q_lo_ready")
        k_ready, k_placed, k_shifted = sem("k_ready"), sem("k_placed"), sem("k_shifted")
        k_hi_ready, k_lo_ready = sem("k_hi_ready"), sem("k_lo_ready")
        v_ready, v1_ready, v_rest_ready = sem("v_ready"), sem("v1_ready"), sem("v_rest_ready")
        v2_ready, v3_ready = sem("v2_ready"), sem("v3_ready")
        kbd_ready = sem("kbd_ready")
        scores_ready = sem("scores_ready")
        masked_ready = sem("masked_ready")
        max_ready = sem("max_ready")
        probs_ready = sem("probs_ready")
        pT_ready, pT_hi_ready, pT_lo_ready = sem("pT_ready"), sem("pT_hi_ready"), sem("pT_lo_ready")
        pv_ready = sem("pv_ready")
        rden_ready = sem("rden_ready")
        head_sum_ready = sem("head_sum_ready")
        heads_ready = sem("heads_ready")
        oT_ready, oT_copied = sem("oT_ready"), sem("oT_copied")
        o_ready = sem("o_ready")
        x1_ready = sem("x1_ready")
        stats2_ready = sem("stats2_ready")
        moments2_ready = sem("moments2_ready")
        var2_ready = sem("var2_ready")
        rstd2_ready = sem("rstd2_ready")
        x2n_ready = sem("x2n_ready")
        x2T_ready, x2hi_ready, x2lo_ready = sem("x2T_ready"), sem("x2hi_ready"), sem("x2lo_ready")
        x1_moved = sem("x1_moved")
        l1_ready, tanh_ready = sem("l1_ready"), sem("tanh_ready")
        silu_ready = sem("silu_ready")
        l1_full, l1_hi, l1_lo = sem("l1_full"), sem("l1_hi"), sem("l1_lo")
        l2_ready, l2_hi, l2_lo = sem("l2_ready"), sem("l2_hi"), sem("l2_lo")
        l3_ready, l3_hi, l3_lo = sem("l3_ready"), sem("l3_hi"), sem("l3_lo")
        l4_ready = sem("l4_ready")
        y_scaled, y_ready = sem("y_scaled"), sem("y_ready")
        y_stored = sem("y_stored")

        block = ctx.enter_context(nc.Block())

        def wait(eng, s, value):
            if not isinstance(value, int) or value > 0:
                eng.wait_ge(s, value)

        def step_bank(kind, k=0):
            return [step[:2] for step in WORK_STEPS].index((kind, k)) % 2

        def before_step(eng, blk, kind, k=0):
            i = [step[:2] for step in WORK_STEPS].index((kind, k))
            n = blk - WORK_STEPS[i][2]
            while True:
                i -= 2
                if i < 0:
                    i += len(WORK_STEPS)
                    n = n - 1
                kind, k, ahead = WORK_STEPS[i]
                if isinstance(n, int) and n < -1:
                    return
                if not isinstance(n, int) or 0 <= n + ahead < BLOCKS:
                    break
            s, per, more = {"S": (masked_ready, NQ, k + 1), "To": (oT_copied, ROWS, k + 1),
                            "O": (x1_ready, ROWS, k + 1), "X2": (x2lo_ready, ROWS, k + 1),
                            "X": (xT_copied, 1, 1), "C": (cT_copied, 1, 1), "Q": (q_lo_ready, 2, 2),
                            "K": (k_shifted, 2, 2), "V": (v_rest_ready, ROWS, k + 1)}[kind]
            wait(eng, s, per * (n + ahead) + more)

        FFN_USES = KF + 2 * PAIRS + ROWS
        assert FFN_USES % 3 == 0 and (GROUPS + 1) % 3 == 0
        L2_USE, L3_USE, L4_USE = KF, KF + PAIRS, KF + 2 * PAIRS

        def ffn_bank(u):
            return u % 3

        def before_ffn(eng, j, u):
            u -= 3
            if u < 0:
                if isinstance(j, int) and j == 0:
                    wait(eng, wT_copied, GROUPS + 1)
                    return
                j, u = j - 1, u + FFN_USES
            if u < L2_USE:
                wait(eng, l1_full, KF * j + (u + 1))
            elif u < L3_USE:
                wait(eng, l2_hi, 4 * PAIRS * j + 4 * (u - L2_USE + 1))
            elif u < L4_USE:
                wait(eng, l3_hi, 4 * PAIRS * j + 4 * (u - L3_USE + 1))
            else:
                wait(eng, y_scaled, ROWS * j + (u - L4_USE + 1))

        @block.sync
        def _(sp):
            def load(n):
                wait(sp, xn_ready, ROWS * n)
                wait(sp, xres_ready, n)
                sp.dma_start(x_in[:], x[bass.ds(n * ROWS, ROWS)].rearrange("b p e -> p b e")).then_inc(x_loaded, 16)
                wait(sp, cT_ready, n)
                sp.dma_start(c_in[:], ctx_in[bass.ds(n * ROWS, ROWS)].rearrange("b p e -> p b e"))\
                    .then_inc(c_loaded, 16)

            def store(j):
                wait(sp, y_ready, ROWS * j + ROWS)
                sp.dma_start(out[bass.ds(j * ROWS, ROWS)].rearrange("b p e -> p b e"), y[:]).then_inc(y_stored, 16)

            def load_chunk(i):
                if i >= 2:
                    wait(sp, wT_ready, 4 * (i - 1) + 1)
                    wait(sp, chunk_tested, min(i - 1, CHUNKS))
                src = chunks[i % CHUNKS][0]
                sp.dma_start(wnat[:, i % 2, :].rearrange("p (o e) -> p o e", o=src.shape[1]), src)\
                    .then_inc(chunk_in[i % 2], 16)

            load(0)
            for w, t in ((Wq, wq), (Wk, wk), (Wv, wv)):
                for kt in range(KE):
                    sp.dma_start(t[:, kt, :].rearrange("p (h d) -> p h d", h=H),
                                 w[:, kt * P:(kt + 1) * P, :].rearrange("h e d -> e h d")).then_inc(attn_w_in, 16)
            for i in range(CHUNKS):
                if i == 4:
                    load(1)
                load_chunk(i)
            sp.wait_ge(flag_ready, 1)
            with sp.If(sp.value_load(flag[0:1, 0:1]) > 0):
                for i in range(CHUNKS, 2 * CHUNKS):
                    load_chunk(i)
            with sp.Fori(1, BLOCKS - 1) as n:
                load(n + 1)
                store(n - 1)
            store(BLOCKS - 2)
            store(BLOCKS - 1)
            sp.wait_ge(y_stored, 16 * BLOCKS)

        @block.gpsimd
        def _(pool):
            pool.memset(ident[:], 0.0).then_inc(pool_const, 1)
            pool.memset(causal[:], 0.0).then_inc(pool_const, 1)
            pool.memset(headmask[:], 1.0).then_inc(pool_const, 1)
            pool.memset(minus_half[:], -0.5).then_inc(pool_const, 1)
            pool.memset(ones[:], 1.0).then_inc(pool_const, 1)
            pool.memset(vs[:], 1.0).then_inc(pool_const, 1)
            pool.wait_ge(pool_const, 6)
            pool.affine_select(out=ident[:], in_=ident[:], compare_op=ALU.not_equal, fill=1.0, base=0,
                               pattern=[[-1, P]], channel_multiplier=1).then_inc(pool_const, 1)
            pool.affine_select(out=causal[:], in_=causal[:], compare_op=ALU.is_ge, fill=MASKED, base=0,
                               pattern=[[0, 4], [-1, P]], channel_multiplier=1).then_inc(pool_const, 1)
            pool.affine_select(out=headmask[:], in_=headmask[:], compare_op=ALU.is_ge, fill=0.0, base=0,
                               pattern=[[-D, HPT]], channel_multiplier=1).then_inc(pool_const, 1)
            pool.wait_ge(pool_const, 9)
            pool.affine_select(out=headmask[:], in_=headmask[:], compare_op=ALU.is_ge, fill=0.0, base=D - 1,
                               pattern=[[D, HPT]], channel_multiplier=-1).then_inc(pool_const, 1)
            pool.wait_ge(pool_const, 10)
            pool.tensor_tensor(quadmask[:], headmask[:, 0:4], headmask[:, 4:8], ALU.add).then_inc(pool_const, 1)
            pool.wait_ge(pool_const, 11)
            def make_kbd(n, t):
                if t == 0:
                    wait(pool, k_lo_ready, n + 1)
                wait(pool, scores_ready, n * NQ + (t - KSLOTS + 1))
                row, m, half = t // QROW, t % QROW // 2, t % 2
                for part, keys in enumerate((k_hi, k_lo)):
                    pool.tensor_tensor(kbd[:, t % KSLOTS, part],
                                       keys[:, half, m, row * P:(row + 1) * P].unsqueeze(1).broadcast_to([P, 4, P]),
                                       quadmask[:].unsqueeze(2).broadcast_to([P, 4, P]), ALU.mult)\
                        .then_inc(kbd_ready, 1)

            def head(n):
                wait(pool, x_loaded, 16 * n + 16)
                wait(pool, x1_ready, ROWS * n)
                if isinstance(n, int) and n == 0:
                    pool.wait_ge(dve_const, 4)
                pool.tensor_tensor(xres[:], x_in[:], bo_tg[:].unsqueeze(1).broadcast_to([P, ROWS, E]), ALU.add)\
                    .then_inc(xres_ready, 1)

            def head_rstd(n):
                wait(pool, var_ready, n + 1)
                pool.tensor_tensor(rstd[:], var_eps[:], minus_half[:], ALU.pow).then_inc(rstd_ready, 1)

            def divide_heads(n, u):
                b, at = u // 2, (u % 2) * PAIR * D
                wait(pool, head_sum_ready, n * (NQ // 2) + u + 1)
                wait(pool, oT_ready, (n - 1) * ROWS + b + 1)
                pool.tensor_tensor(heads[:, b, at:at + PAIR * D].rearrange("p (h d) -> p h d", h=PAIR),
                                   head_sum[:, u % 2],
                                   rden[:, b, (u % 2) * PAIR:(u % 2 + 1) * PAIR].unsqueeze(2)
                                   .broadcast_to([P, PAIR, D]), ALU.mult)\
                    .then_inc(heads_ready, 1)

            def split_values(n, b):
                rest = v_rest[:, b].rearrange("p (h d) -> p h d", h=H)
                wait(pool, v2_ready, ROWS * n + b + 1)
                pool.tensor_tensor(vs[:, b, :, 2 * D:3 * D], rest, vs[:, b, :, D:2 * D], ALU.subtract)\
                    .then_inc(v3_ready, 1)

            def body(n, ffn_on=True, attn=True, next_head=True):
                j = n - 1
                for kind, k, ahead in ORDER:
                    blk = n + ahead
                    here = next_head if ahead else attn
                    if kind == "l" and ffn_on:
                        wait(pool, l1_hi, j * KF + k + 1)
                        pool.tensor_tensor(ha_lo[:, k], full[:, k % 4], ha_hi[:, k], ALU.subtract)\
                            .then_inc(l1_lo, 1)
                    if kind == "kb" and here:
                        make_kbd(blk, k)
                    if kind == "n2" and here:
                        wait(pool, var2_ready, blk * ROWS + k + 1)
                        pool.tensor_tensor(rstd2[:, k:k + 1], var_eps2[:, k:k + 1], minus_half[:, 0:1], ALU.pow)\
                            .then_inc(rstd2_ready, 1)
                    if kind == "nm" and here:
                        divide_heads(blk, k)
                    if kind == "z" and ffn_on:
                        wait(pool, y_scaled, ROWS * j + k + 1)
                        pool.tensor_tensor(y[:, k], y[:, k], x1_prev[:, k], ALU.add).then_inc(y_ready, 1)
                    if kind == "st" and here:
                        head_rstd(blk)
                    if kind == "rx" and here:
                        head(blk)
                    if kind == "v" and here:
                        split_values(blk, k)

            body(-1, ffn_on=False, attn=False)
            body(0, ffn_on=False)
            body(1)
            with pool.Fori(2, BLOCKS - 1) as n:
                body(n)
            body(BLOCKS - 1, next_head=False)
            body(BLOCKS, attn=False, next_head=False)

        @block.vector
        def _(dve):
            dve.wait_ge(pool_const, 10)

            def scale_constants():
                dve.wait_ge(scales_in, 6 * 16)
                dve.tensor_scalar(half_s1[:], s1_col[:], 0.5, None, ALU.mult).then_inc(dve_const, 1)
                dve.wait_ge(dve_const, 1)
                dve.tensor_tensor(half_s12[:], half_s1[:], s2_col[:], ALU.mult).then_inc(dve_const, 1)
                dve.wait_ge(gates_ready, 1)
                dve.tensor_scalar(bo_tg[:], bo_tg[:], gates[:, 0:1], None, ALU.mult).then_inc(dve_const, 1)
                dve.tensor_scalar(s3_tg[:], s3_tg[:], gates[:, 1:2], None, ALU.mult).then_inc(dve_const, 1)

            def hold_wait():
                dve.memset(wait_holder[:], 0.0)

            def head_stats(n):
                wait(dve, x_loaded, 16 * n + 16)
                for b in range(ROWS):
                    dve.bn_stats(stats[:, b], x_in[:, b]).then_inc(stats_ready, 1)
                wait(dve, stats_ready, ROWS * n + ROWS)
                hold_wait()
                for b in range(ROWS):
                    dve.bn_aggr(moments[:, b], stats[:, b]).then_inc(moments_ready, 1)
                wait(dve, moments_ready, ROWS * n + ROWS)
                dve.tensor_scalar(var_eps[:], moments[:, :, 1], EPS, None, ALU.add).then_inc(var_ready, 1)

            def head_norm(n):
                wait(dve, rstd_ready, n + 1)
                wait(dve, xT_ready, n)
                for b in range(ROWS):
                    dve.tensor_scalar(xn[:, b], x_in[:, b], moments[:, b, 0:1], rstd[:, b:b + 1],
                                      ALU.subtract, ALU.mult).then_inc(xn_ready, 1)

            def keys(n):
                src = work[step_bank("K")][:].rearrange("p (m t) -> p m t", m=KE)
                wait(dve, k_placed, 2 * n + 2)
                dve.tensor_copy(k_lo[HALF:P, 0], src[0:HALF]).then_inc(k_shifted, 1)
                dve.tensor_copy(k_lo[0:HALF, 1], src[HALF:P]).then_inc(k_shifted, 1)
                wait(dve, k_shifted, 2 * n + 2)
                dve.tensor_copy(k_hi[:], k_lo[:]).then_inc(k_hi_ready, 1)
                wait(dve, k_hi_ready, n + 1)
                dve.tensor_tensor(k_lo[:], k_lo[:], k_hi[:].bitcast(F32), ALU.subtract).then_inc(k_lo_ready, 1)

            def queries(n):
                src = work[step_bank("Q")][:].rearrange("p (m t) -> p m t", m=KE)
                wait(dve, q_hi_ready, 2 * n + 2)
                dve.tensor_tensor(qs[HALF:P, 0], src[0:HALF], qs[0:HALF, 0].bitcast(F32), ALU.subtract)\
                    .then_inc(q_lo_ready, 1)
                dve.tensor_tensor(qs[0:HALF, 1], src[HALF:P], qs[HALF:P, 1].bitcast(F32), ALU.subtract)\
                    .then_inc(q_lo_ready, 1)

            def values(n, b):
                use = step_bank("V", b)
                wait(dve, v3_ready, ROWS * (n - 1) + b + 1)
                wait(dve, v1_ready, ROWS * n + b + 1)
                dve.tensor_tensor(v_rest[:, b].rearrange("p (h d) -> p h d", h=H),
                                  work[use][:, 0:E].rearrange("p (h d) -> p h d", h=H), vs[:, b, :, 0:D],
                                  ALU.subtract).then_inc(v_rest_ready, 1)
                wait(dve, v_rest_ready, ROWS * n + b + 1)
                dve.tensor_copy(vs[:, b, :, D:2 * D], v_rest[:, b].rearrange("p (h d) -> p h d", h=H))\
                    .then_inc(v2_ready, 1)

            def mask(n, t):
                use = step_bank("S", t)
                slot = t % PSLOTS
                wait(dve, scores_ready, n * NQ + t + 1)
                wait(dve, pT_ready, n * NQ + (t - PSLOTS + 1))
                dve.scalar_tensor_tensor(probs[:, slot], work[use][:].rearrange("p (h t) -> p h t", h=4), SCALE,
                                         causal[:], ALU.mult, ALU.add)\
                    .then_inc(masked_ready, 1)

            def maximum(n, t):
                slot = t % PSLOTS
                wait(dve, masked_ready, n * NQ + t + 1)
                dve.tensor_reduce(negmax[:, slot], probs[:, slot], AX_X, ALU.max, negate=True).then_inc(max_ready, 1)

            def pT_low(n, t):
                wait(dve, pT_hi_ready, n * NQ + t + 1)
                dve.scalar_tensor_tensor(pT_lo[:, t % 2], pT_bank[:].rearrange("p (h t) -> p h t", h=4), PT_SCALE,
                                         pT_hi[:, t % 2], ALU.mult, ALU.subtract).then_inc(pT_lo_ready, 1)

            def normalise(n, u):
                o = pv[u % 2][:, 0:PAIR * VCOLS].rearrange("p (h d) -> p h d", h=PAIR)
                b = u // 2
                wait(dve, pv_ready, n * NQ + 2 * u + 2)
                wait(dve, heads_ready, n * (NQ // 2) + (u - 1))
                dve.reciprocal(rden[:, b, (u % 2) * PAIR:(u % 2 + 1) * PAIR], o[:, :, PARTS * D])\
                    .then_inc(rden_ready, 1)
                dve.tensor_reduce(head_sum[:, u % 2], o[:, :, 0:PARTS * D].rearrange("p h (c d) -> p h d c", c=PARTS),
                                  AX_X, ALU.add).then_inc(head_sum_ready, 1)

            def l1_silu(j, m):
                f = full[:, m % 4]
                wait(dve, tanh_ready, j * KF + m + 1)
                dve.scalar_tensor_tensor(f, f, 1.0, ffn[ffn_bank(m)][:, 0:TOK], ALU.add, ALU.mult)\
                    .then_inc(silu_ready, 1)

            def l1_product(j, m):
                f = full[:, m % 4]
                wait(dve, silu_ready, j * KF + m + 1)
                dve.scalar_tensor_tensor(f, ffn[ffn_bank(m)][:, TOK:2 * TOK], half_s12[:, m:m + 1], f,
                                         ALU.mult, ALU.mult).then_inc(l1_full, 1)

            def lows(j, p, hi_sem, hi, lo, lo_sem):
                wait(dve, hi_sem, (j * PAIRS + p + 1) * 4)
                f = full[:, 2 * (p % 2):2 * (p % 2) + 2]
                dve.tensor_tensor(lo[:, 2 * p:2 * p + 2], f, hi[:, 2 * p:2 * p + 2], ALU.subtract)\
                    .then_inc(lo_sem, 1)

            def body(n, ffn_on=True, attn=True, next_head=True, weights=False):
                j = n - 1
                for kind, k, ahead in ORDER:
                    blk = n + ahead
                    here = next_head if ahead else attn
                    if kind == "s" and here:
                        mask(blk, k)
                    if kind == "m" and here:
                        maximum(blk, k)
                    if kind == "u" and here:
                        pT_low(blk, k)
                    if kind == "nh" and here:
                        normalise(blk, k)
                    if kind == "g" and ffn_on:
                        l1_silu(j, k)
                    if kind == "f" and ffn_on:
                        l1_product(j, k)
                    if kind == "mv" and ffn_on:
                        wait(dve, y_ready, ROWS * j)
                        wait(dve, x2n_ready, ROWS * j + ROWS)
                        dve.tensor_copy(x1_prev[:], x1[:]).then_inc(x1_moved, 1)
                    if kind == "W" and weights:
                        dve.wait_ge(chunk_in[k % 2], 16 * (k // 2 + 1))
                        wait(dve, chunk_tested, k)
                        w_bits = wnat[:, k % 2].bitcast(I32)
                        if k == 0:
                            dve.tensor_scalar(wlow[:], w_bits, LOW_BITS, None, ALU.bitwise_and)\
                                .then_inc(chunk_tested, 1)
                        else:
                            dve.scalar_tensor_tensor(wlow[:], w_bits, LOW_BITS, wlow[:], ALU.bitwise_and,
                                                     ALU.bitwise_or).then_inc(chunk_tested, 1)
                    if kind == "W" and weights and k == CHUNKS - 1:
                        dve.wait_ge(chunk_tested, CHUNKS)
                        dve.tensor_reduce(low_all[:], wlow[:], AX_X, ALU.max).then_inc(flag_steps, 1)
                        dve.wait_ge(flag_steps, 1)
                        dve.tensor_scalar(inexact[:], low_all[:], 1.0, None, ALU.min).then_inc(flag_steps, 1)
                    if kind == "st" and here:
                        head_stats(blk)
                    if kind == "nx" and here:
                        head_norm(blk)
                    if kind == "nx" and isinstance(n, int) and n == -1:
                        scale_constants()
                    if kind == "w2" and ffn_on:
                        lows(j, k, l2_hi, hb_hi, hb_lo, l2_lo)
                    if kind == "w3" and ffn_on:
                        lows(j, k, l3_hi, ha_hi, ha_lo, l3_lo)
                    if kind == "y" and ffn_on:
                        use = ffn_bank(L4_USE + k)
                        wait(dve, l4_ready, ROWS * j + k + 1)
                        wait(dve, y_stored, 16 * j)
                        dve.tensor_tensor(y[:, k], ffn[use][:, 0:E], s3_tg[:], ALU.mult)\
                            .then_inc(y_scaled, 1)
                    if kind == "o" and here:
                        use = step_bank("O", k)
                        wait(dve, o_ready, blk * ROWS + k + 1)
                        wait(dve, xres_ready, blk + 1)
                        wait(dve, x1_moved, blk)
                        dve.scalar_tensor_tensor(x1[:, k], work[use][:, 0:E], gates[:, 0:1], xres[:, k],
                                                 ALU.mult, ALU.add).then_inc(x1_ready, 1)
                        wait(dve, x1_ready, blk * ROWS + k + 1)
                        dve.bn_stats(stats2[:, k], x1[:, k]).then_inc(stats2_ready, 1)
                        wait(dve, stats2_ready, blk * ROWS + k + 1)
                        hold_wait()
                        dve.bn_aggr(moments2[:, k], stats2[:, k]).then_inc(moments2_ready, 1)
                        wait(dve, moments2_ready, blk * ROWS + k + 1)
                        dve.tensor_scalar(var_eps2[:, k:k + 1], moments2[:, k, 1:2], EPS, None, ALU.add)\
                            .then_inc(var2_ready, 1)
                    if kind == "n2" and here:
                        wait(dve, rstd2_ready, blk * ROWS + k + 1)
                        wait(dve, x2T_ready, (blk - 1) * ROWS + k + 1)
                        dve.tensor_scalar(x2n[:, k], x1[:, k], moments2[:, k, 0:1], rstd2[:, k:k + 1],
                                          ALU.subtract, ALU.mult).then_inc(x2n_ready, 1)
                    if kind == "x2" and here:
                        use = step_bank("X2", k)
                        wait(dve, x2hi_ready, blk * ROWS + k + 1)
                        dve.tensor_tensor(x2T_lo[:, :, k * P:(k + 1) * P],
                                          work[use][:, 0:E].rearrange("p (m t) -> p m t", m=KE),
                                          x2T_hi[:, :, k * P:(k + 1) * P], ALU.subtract)\
                            .then_inc(x2lo_ready, 1)
                    if kind == "q" and here:
                        queries(blk)
                    if kind == "k" and here:
                        keys(blk)
                    if kind == "v" and here:
                        values(blk, k)

            body(-1, ffn_on=False, attn=False)
            body(0, ffn_on=False, weights=True)
            dve.wait_ge(flag_sum, 1)
            dve.tensor_copy(flag[:], pT_bank[0:1, 0:1]).then_inc(flag_ready, 1)
            body(1)
            with dve.Fori(2, BLOCKS - 1) as n:
                body(n)
            body(BLOCKS - 1, next_head=False)
            body(BLOCKS, attn=False, next_head=False)

        @block.scalar
        def _(act):
            act.dma_start(gates_in[:, 0:1], g_xattn.rearrange("(a n) -> a n", a=1).partition_broadcast(P))\
                .then_inc(gates_loaded, 16)
            act.dma_start(gates_in[:, 1:2], g_ffn.rearrange("(a n) -> a n", a=1).partition_broadcast(P))\
                .then_inc(gates_loaded, 16)
            act.dma_start(bo_tg[:], bo.rearrange("(a n) -> a n", a=1).partition_broadcast(P))\
                .then_inc(scales_in, 16)
            act.dma_start(s3_tg[:], w3s.rearrange("(a n) -> a n", a=1).partition_broadcast(P))\
                .then_inc(scales_in, 16)
            for s, t in ((s1, s1_col), (s2, s2_col), (h1s, h1s_col), (h2s, h2s_col)):
                act.dma_start(t[:], s.rearrange("(m p) -> p m", p=P), allow_slow_non_contiguous=True).then_inc(scales_in, 16)
            act.dma_start(wo_nat[:], Wo.rearrange("(o p) e -> p o e", p=P)).then_inc(wo_in, 16)
            act.wait_ge(gates_loaded, 32)
            act.activation(gates[:], gates_in[:], ACT.Tanh).then_inc(gates_ready, 1)

            def copy_wT(i):
                act.wait_ge(wT_ready, i + 1)
                if i == 0:
                    dst = woT[:].rearrange("p k e -> p (k e)")
                elif i <= GROUPS:
                    at = groups[i - 1][2]
                    dst = W[:, at:at + BANK]
                else:
                    g = i - GROUPS
                    if g > 4:
                        act.wait_ge(stage_saved[g % 4], 16 * ((g - 1) // 4))
                    dst = wstage[:, g % 4]
                act.activation(dst, ffn[i % 3][:], ACT.Copy).then_inc(wT_copied, 1)

            def save_wT(g):
                at = groups[g - 1][2]
                act.wait_ge(wT_copied, GROUPS + g + 1)
                act.dma_start(W[:, at:at + BANK].bitcast(F32), wstage[:, g % 4]).then_inc(stage_saved[g % 4], 16)

            def head_step(n, kind):
                use = step_bank(kind.upper())
                src = work[use][:].rearrange("p (m t) -> p m t", m=KE)
                if kind == "x":
                    wait(act, xT_ready, n + 1)
                    wait(act, q_ready, n)
                    act.activation(xT[:], src, ACT.Copy).then_inc(xT_copied, 1)
                if kind == "c":
                    wait(act, cT_ready, n + 1)
                    wait(act, v_ready, ROWS * n)
                    act.activation(cT[:], src, ACT.Copy).then_inc(cT_copied, 1)
                if kind == "q":
                    wait(act, q_ready, n + 1)
                    wait(act, scores_ready, NQ * n)
                    act.activation(qs[0:HALF, 0], src[0:HALF], ACT.Copy).then_inc(q_hi_ready, 1)
                    act.activation(qs[HALF:P, 1], src[HALF:P], ACT.Copy).then_inc(q_hi_ready, 1)
                if kind == "k":
                    wait(act, k_ready, n + 1)
                    wait(act, kbd_ready, 2 * NQ * n)
                    act.activation(k_lo[0:HALF, 0], src[0:HALF], ACT.Copy).then_inc(k_placed, 1)
                    act.activation(k_lo[HALF:P, 1], src[HALF:P], ACT.Copy).then_inc(k_placed, 1)

            def exps(n, t):
                slot = t % PSLOTS
                wait(act, max_ready, n * NQ + t + 1)
                for h in range(4):
                    last = act.activation(probs[:, slot, h], probs[:, slot, h], ACT.Exp,
                                          bias=negmax[:, slot, h:h + 1])
                last.then_inc(probs_ready, 1)

            def pT_high(n, t):
                wait(act, pT_ready, n * NQ + t + 1)
                wait(act, pv_ready, n * NQ + (t - 1))
                act.activation(pT_hi[:, t % 2], pT_bank[:].rearrange("p (h t) -> p h t", h=4), ACT.Copy,
                               scale=PT_SCALE).then_inc(pT_hi_ready, 1)

            def values(n, b):
                use = step_bank("V", b)
                wait(act, v_ready, ROWS * n + b + 1)
                wait(act, pv_ready, NQ * n)
                act.activation(vs[:, b, :, 0:D], work[use][:, 0:E].rearrange("p (h d) -> p h d", h=H), ACT.Copy)\
                    .then_inc(v1_ready, 1)

            def gelus(j, m, first_use, ready, scales, hi, hi_sem):
                p, r = m // 2, m % 2
                use = ffn_bank(first_use + p)
                src = ffn[use][:, r * TOK:(r + 1) * TOK]
                wait(act, ready, j * KF + 2 * p + 2)
                act.activation(full[:, 2 * (p % 2) + r], src, ACT.Gelu, scale=scales[:, m:m + 1])\
                    .then_inc(hi_sem, 1)
                act.activation(hi[:, m], src, ACT.Gelu, scale=scales[:, m:m + 1]).then_inc(hi_sem, 1)

            def body(n, ffn_on=True, attn=True, next_head=True, weights=False):
                j = n - 1
                for kind, k, ahead in ORDER:
                    blk = n + ahead
                    here = next_head if ahead else attn
                    if kind == "e" and here:
                        exps(blk, k)
                    if kind == "t" and here:
                        pT_high(blk, k)
                    if kind == "h" and ffn_on:
                        wait(act, l1_full, j * KF + k + 1)
                        if k == 0:
                            wait(act, l4_ready, ROWS * j)
                        act.activation(ha_hi[:, k], full[:, k % 4], ACT.Copy).then_inc(l1_hi, 1)
                    if kind == "a1" and ffn_on:
                        use = ffn_bank(k)
                        wait(act, l1_ready, j * KF + k + 1)
                        if k < 4:
                            wait(act, l3_lo, PAIRS * j)
                        else:
                            wait(act, l1_lo, j * KF + (k - 3))
                        act.activation(full[:, k % 4], ffn[use][:, 0:TOK], ACT.Tanh, scale=half_s1[:, k:k + 1])\
                            .then_inc(tanh_ready, 1)
                    if kind == "W" and weights:
                        for g in range(4 * k + 1, 4 * k + 5):
                            copy_wT(g)
                    if kind == "a2" and ffn_on:
                        p = k // 2
                        if k % 2 == 0:
                            if p < 2:
                                wait(act, l1_lo, j * KF + KF - 2 + 2 * p)
                            else:
                                wait(act, l2_lo, j * PAIRS + (p - 1))
                        if k == 0:
                            wait(act, l3_ready, j * KF)
                        gelus(j, k, L2_USE, l2_ready, h1s_col, hb_hi, l2_hi)
                    if kind == "a3" and ffn_on:
                        p = k // 2
                        if k % 2 == 0:
                            if p < 2:
                                wait(act, l2_lo, j * PAIRS + (PAIRS - 1 + p))
                            else:
                                wait(act, l3_lo, j * PAIRS + (p - 1))
                        if k == 0:
                            wait(act, l2_ready, j * KF + KF)
                        gelus(j, k, L3_USE, l3_ready, h2s_col, ha_hi, l3_hi)
                    if kind == "to" and here:
                        use = step_bank("To", k)
                        wait(act, oT_ready, blk * ROWS + k + 1)
                        wait(act, o_ready, (blk - 1) * ROWS + k + 1)
                        act.activation(oT[:, :, k * P:(k + 1) * P],
                                       work[use][:, 0:E].rearrange("p (m t) -> p m t", m=KE), ACT.Copy)\
                            .then_inc(oT_copied, 1)
                    if kind == "x2" and here:
                        use = step_bank("X2", k)
                        wait(act, x2T_ready, blk * ROWS + k + 1)
                        wait(act, l1_ready, KF * blk)
                        act.activation(x2T_hi[:, :, k * P:(k + 1) * P],
                                       work[use][:, 0:E].rearrange("p (m t) -> p m t", m=KE), ACT.Copy)\
                            .then_inc(x2hi_ready, 1)
                    if kind in ("x", "c", "q", "k") and here:
                        head_step(blk, kind)
                    if kind == "v" and here:
                        values(blk, k)

            body(-1, ffn_on=False, attn=False)
            copy_wT(0)
            act.wait_ge(scales_in, 6 * 16)
            act.wait_ge(dve_const, 1)
            body(0, ffn_on=False, weights=True)
            act.wait_ge(flag_ready, 1)
            with act.If(act.value_load(flag[0:1, 0:1]) > 0):
                for g in range(1, GROUPS + 1):
                    copy_wT(GROUPS + g)
                    save_wT(g)
            body(1)
            with act.Fori(2, BLOCKS - 1) as n:
                body(n)
            body(BLOCKS - 1, next_head=False)
            body(BLOCKS, attn=False, next_head=False)

        @block.tensor
        def _(pe):
            def transpose_w(i):
                wait(pe, wT_copied, i - 2)
                if i == 0:
                    pe.wait_ge(wo_in, 16)
                    tiles = [wo_nat[:, o, kt * P:(kt + 1) * P] for kt in range(KE) for o in range(KE)]
                else:
                    arrival = (i - 1) // 4
                    c, where, _ = groups[(i - 1) % GROUPS]
                    slot = arrival % 2
                    pe.wait_ge(chunk_in[slot], 16 * (arrival // 2 + 1))
                    width = chunks[c][0].shape[2]
                    nat = wnat[:, slot, :].rearrange("p (o e) -> p o e", e=width)
                    tiles = [nat[:, o, e:e + P] for o, e in where]
                for r, tile in enumerate(tiles):
                    last = pe.transpose(ffn[i % 3][:, r * P:(r + 1) * P], tile, ident[:])
                last.then_inc(wT_ready, 1)

            def project(dst, lhsT, rhs):
                for kt in range(KE):
                    last = pe.matmul(dst, lhsT(kt), rhs(kt), start=kt == 0, stop=kt == KE - 1)
                return last

            def head_step(n, kind, k):
                bank_ = work[step_bank(kind, k)]
                before_step(pe, n, kind, k)
                if kind == "X":
                    wait(pe, xn_ready, ROWS * n + ROWS)
                    for kt in range(KE):
                        for b in range(ROWS):
                            last = pe.transpose(bank_[:, (kt * ROWS + b) * P:(kt * ROWS + b + 1) * P],
                                                xn[:, b, kt * P:(kt + 1) * P], ident[:])
                    last.then_inc(xT_ready, 1)
                if kind == "C":
                    wait(pe, c_loaded, 16 * n + 16)
                    for kt in range(KE):
                        for b in range(ROWS):
                            last = pe.transpose(bank_[:, (kt * ROWS + b) * P:(kt * ROWS + b + 1) * P],
                                                c_in[:, b, kt * P:(kt + 1) * P], ident[:])
                    last.then_inc(cT_ready, 1)
                if kind in ("Q", "K"):
                    if isinstance(n, int) and n == 0:
                        pe.wait_ge(attn_w_in, 3 * KE * 16)
                    w, src = (wq, xT) if kind == "Q" else (wk, cT)
                    wait(pe, xT_copied if kind == "Q" else cT_copied, n + 1)
                    for m in range(KE):
                        last = project(bank_[:, m * TOK:(m + 1) * TOK], lambda kt: w[:, kt, m * P:(m + 1) * P],
                                       lambda kt: src[:, kt])
                    last.then_inc(q_ready if kind == "Q" else k_ready, 1)
                if kind == "V":
                    project(bank_[:, 0:E], lambda kt: cT[:, kt, k * P:(k + 1) * P], lambda kt: wv[:, kt])\
                        .then_inc(v_ready, 1)

            def scores(n, t):
                use = step_bank("S", t)
                row, m, half = t // QROW, t % QROW // 2, t % 2
                before_step(pe, n, "S", t)
                if t == 0:
                    wait(pe, q_lo_ready, 2 * n + 2)
                wait(pe, kbd_ready, 2 * (n * NQ + t + 1))
                for part in range(2):
                    last = pe.matmul(work[use][:], qs[:, half, m, row * P:(row + 1) * P], kbd[:, t % KSLOTS, part],
                                     start=part == 0, stop=part == 1)
                last.then_inc(scores_ready, 1)

            def transpose_probs(n, t):
                wait(pe, probs_ready, n * NQ + t + 1)
                wait(pe, pT_lo_ready, n * NQ + t)
                for h in range(4):
                    last = pe.transpose(pT_bank[:, h * P:(h + 1) * P], probs[:, t % PSLOTS, h], ident[:])
                last.then_inc(pT_ready, 1)

            def probs_values(n, t):
                row, u = t // QROW, t // 2
                wait(pe, pT_lo_ready, n * NQ + t + 1)
                if t % QROW == 0:
                    wait(pe, v3_ready, n * ROWS + row + 1)
                if t % 2 == 0:
                    wait(pe, head_sum_ready, n * (NQ // 2) + (u - 1))
                for i in range(4):
                    h, at = 4 * (t % QROW) + i, (4 * (t % 2) + i) * VCOLS
                    for part in (pT_hi, pT_lo):
                        last = pe.matmul(pv[u % 2][:, at:at + VCOLS], part[:, t % 2, i], vs[:, row, h],
                                         start=part is pT_hi, stop=part is pT_lo)
                last.then_inc(pv_ready, 1)

            def run(general, first):
                def mm(dst, w, h, **flags):
                    if general:
                        w, h = w.bitcast(F32), h.bitcast(F32)
                    return pe.matmul(dst, w, h, **flags)

                def hidden(dst, weight_at, tiles, m, his, los, out_width, before_tile=lambda kt: None):
                    n_mm = 2 * tiles
                    i = 0
                    for kt in range(tiles):
                        before_tile(kt)
                        for part in (his, los):
                            at = weight_at + kt * out_width + m * P
                            last = mm(dst, W[:, at:at + P], part[:, kt], start=i == 0, stop=i == n_mm - 1)
                            i += 1
                    return last

                def body(n, ffn_on=True, attn=True, next_head=True, weights=False):
                    j = n - 1

                    def tile_split(kt):
                        wait(pe, l1_lo, KF * j + kt + 1)

                    def pair_split(lo_sem):
                        def before_tile(kt):
                            if kt % 2 == 0:
                                wait(pe, lo_sem, PAIRS * j + kt // 2 + 1)
                        return before_tile

                    for kind, k, ahead in ORDER:
                        blk = n + ahead
                        here = next_head if ahead else attn
                        if kind == "L1" and ffn_on:
                            use = ffn_bank(k)
                            before_ffn(pe, j, k)
                            if k == 0:
                                wait(pe, x2lo_ready, ROWS * j + ROWS)
                            hidden(ffn[use][:, 0:TOK], W1_AT, KE, k, x2T_hi, x2T_lo, F)
                            hidden(ffn[use][:, TOK:2 * TOK], W2_AT, KE, k, x2T_hi, x2T_lo, F).then_inc(l1_ready, 1)
                        if kind in ("L2", "L3") and ffn_on:
                            first_use, at, his, los, out_width, ready, split = {
                                "L2": (L2_USE, H1_AT, ha_hi, ha_lo, F, l2_ready, tile_split),
                                "L3": (L3_USE, H2_AT, hb_hi, hb_lo, F, l3_ready, pair_split(l2_lo))}[kind]
                            use, r = ffn_bank(first_use + k // 2), k % 2
                            if r == 0:
                                before_ffn(pe, j, first_use + k // 2)
                            dst = ffn[use][:, r * TOK:(r + 1) * TOK]
                            if k == 0:
                                last = hidden(dst, at, KF, k, his, los, out_width, split)
                            else:
                                last = hidden(dst, at, KF, k, his, los, out_width)
                            last.then_inc(ready, 1)
                        if kind == "L4" and ffn_on:
                            if k == 0:
                                for b in range(ROWS):
                                    before_ffn(pe, j, L4_USE + b)
                            for kt in (2 * k, 2 * k + 1):
                                pair_split(l3_lo)(kt)
                                for b in range(ROWS):
                                    dst = ffn[ffn_bank(L4_USE + b)][:, 0:E]
                                    for i, part in enumerate((ha_hi, ha_lo)):
                                        last = mm(dst, part[:, kt, b * P:(b + 1) * P],
                                                  W[:, W3_AT + kt * E:W3_AT + (kt + 1) * E],
                                                  start=kt == 0 and i == 0, stop=kt == KF - 1 and i == 1)
                                    if kt == KF - 1:
                                        last.then_inc(l4_ready, 1)
                        if kind == "S" and here:
                            scores(blk, k)
                        if kind == "T" and here:
                            transpose_probs(blk, k)
                        if kind == "PV" and here:
                            probs_values(blk, k)
                        if kind == "W" and weights:
                            for g in range(4 * k + 1, 4 * k + 5):
                                transpose_w(g)
                        if kind in ("To", "O", "X2") and here:
                            use = step_bank(kind, k)
                            before_step(pe, blk, kind, k)
                            if kind == "O":
                                wait(pe, oT_copied, blk * ROWS + k + 1)
                                project(work[use][:, 0:E], lambda kt: oT[:, kt, k * P:(k + 1) * P],
                                        lambda kt: woT[:, kt]).then_inc(o_ready, 1)
                            else:
                                if kind == "To":
                                    src, done = heads, oT_ready
                                    wait(pe, heads_ready, blk * (NQ // 2) + 2 * k + 2)
                                else:
                                    src, done = x2n, x2T_ready
                                    wait(pe, x2n_ready, blk * ROWS + k + 1)
                                for kt in range(KE):
                                    last = pe.transpose(work[use][:, kt * P:(kt + 1) * P],
                                                        src[:, k, kt * P:(kt + 1) * P], ident[:])
                                last.then_inc(done, 1)
                        if kind in HEAD_WORK and here:
                            head_step(blk, kind, k)
                    if weights:
                        pe.wait_ge(flag_steps, 2)
                        pe.wait_ge(pT_lo_ready, NQ)
                        pe.matmul(pT_bank[0:1, 0:1], inexact[:], ones[:], start=True, stop=True).then_inc(flag_sum, 1)

                if first == 0:
                    body(-1, ffn_on=False, attn=False)
                    transpose_w(0)
                    body(0, ffn_on=False, weights=True)
                    return
                body(1)
                with pe.Fori(2, BLOCKS - 1) as n:
                    body(n)
                body(BLOCKS - 1, next_head=False)
                body(BLOCKS, attn=False, next_head=False)

            pe.wait_ge(pool_const, 10)
            run(False, 0)
            pe.wait_ge(flag_ready, 1)
            any_inexact = pe.value_load(flag[0:1, 0:1])
            with pe.If(any_inexact > 0):
                for i in range(GROUPS + 1, 2 * GROUPS + 1):
                    transpose_w(i)
                for saved in stage_saved:
                    pe.wait_ge(saved, 16 * (GROUPS // 4))
                run(True, 1)
            with pe.Else():
                run(False, 1)


_INS = ["x", "ctx_1024", "g_xattn", "g_ffn", "L0_xattn_Wq", "L0_xattn_Wk", "L0_xattn_Wv", "L0_xattn_Wo",
        "L0_xattn_bo", "L0_ffn_w1_w", "L0_ffn_w1_s", "L0_ffn_w2_w", "L0_ffn_w2_s", "L0_ffn_h1_w", "L0_ffn_h1_s",
        "L0_ffn_h2_w", "L0_ffn_h2_s", "L0_ffn_w3_w", "L0_ffn_w3_s"]


def kernel(**inputs):
    import numpy as np
    import concourse.bacc as bacc
    from concourse.bass_utils import run_bass_kernel_spmd

    nc = bacc.Bacc("TRN2", target_bir_lowering=False, num_devices=1)
    arrays, args = {}, []
    for name in _INS:
        a = np.ascontiguousarray(inputs[name])
        arrays[f"in_{name}"] = a
        args.append(nc.dram_tensor(f"in_{name}", a.shape, mybir.dt.from_np(a.dtype), kind="ExternalInput").ap())
    shape = arrays["in_x"].shape
    args.append(nc.dram_tensor("out", shape, F32, kind="ExternalOutput").ap())
    program(nc, *args)
    result = run_bass_kernel_spmd(nc, [arrays], core_ids=[0])
    return result.results[0]["out"]
```
